# Optimizing a Trainium2 kernel written in Bass

```python
import numpy as np
import jax
import jax.numpy as jnp

def _softmax(x, axis=-1):
    return jax.nn.softmax(x, axis=axis)

def _gelu(x):
    return jax.nn.gelu(x, approximate=True)

def _silu(x):
    return jax.nn.silu(x)

def _sigmoid(x):
    return jax.nn.sigmoid(x)

def _layernorm(x, axis=-1, eps=1e-05):
    m = jnp.mean(x, axis=axis, keepdims=True)
    v = jnp.var(x, axis=axis, keepdims=True)
    return (x - m) / jnp.sqrt(v + eps)

def _scatter_add(tgt, idx, src, axis=0):
    return tgt.at[idx].add(src)

def _segment_sum(src, seg, n):
    return jax.ops.segment_sum(src, seg, n)
kernel_name = 'mk_adj_resnorm_d2_adj_r2_407047'

def setup_inputs(seed: int=0):
    np.random.seed(seed)
    _w = jnp.asarray

    def _rec_inputs():
        import jax
        import jax.numpy as jnp
        _gk = jax.random.key(seed)
        x = -0.0002928 + 1 * jax.random.normal(jax.random.fold_in(_gk, 1), (8, 1024, 128), jnp.float32)
        _a = jax.random.bernoulli(jax.random.fold_in(_gk, 2), 0.015625, (1024, 1024))
        _a = jnp.logical_or(_a, jnp.swapaxes(_a, -1, -2))
        _a = jnp.logical_or(_a, jnp.eye(1024, dtype=bool))
        adj = _a.astype(jnp.int32)
        return (x, adj)
    x, adj = _rec_inputs()

    def _L0_gnn_setup():
        import jax, jax.numpy as jnp
        import numpy as np
        ALPHA = 0.2
        NEG_INF = -9000000000000000.0

        def _gat(inp, adj_mask, W, a):
            h = jnp.matmul(inp, W)
            F_ = h.shape[-1]
            f1 = jnp.matmul(h, a[:F_, 0])
            f2 = jnp.matmul(h, a[F_:, 0])
            e = jax.nn.leaky_relu(f1[:, :, None] + f2[:, None, :], ALPHA)
            if adj_mask is not None:
                e = jnp.where(adj_mask[None, :, :] > 0, e, NEG_INF)
            att = jax.nn.softmax(e, axis=2)
            h_prime = jnp.einsum('bij,bjf->bif', att, h)
            return jax.nn.elu(h_prime)
        key = jax.random.key(seed)
        ks = jax.random.split(key, 10)
        B, N, Fin, H, O = (16, 512, 128, 256, 128)

        def xavier(k, shape):
            fan_in, fan_out = (shape[0], shape[-1])
            bound = 1.414 * np.sqrt(6.0 / (fan_in + fan_out))
            return jax.random.uniform(k, shape, jnp.float32, -bound, bound)
        return {'x': jax.random.normal(ks[0], (B, N, Fin), jnp.float32), 'adj': jax.random.randint(ks[1], (N, N), 0, 2, jnp.int32), 'mlp1_w': xavier(ks[2], (Fin, H)), 'mlp1_b': jnp.zeros((H,), jnp.float32), 'mlp2_w': xavier(ks[3], (H, O)), 'mlp2_b': jnp.zeros((O,), jnp.float32), 'W_fc': xavier(ks[4], (H, H)), 'a_fc': xavier(ks[5], (2 * H, 1)), 'W_hand': xavier(ks[6], (O, O)), 'a_hand': xavier(ks[7], (2 * O, 1))}
    _L0_gnn_all = _L0_gnn_setup()
    _L0_gnn_in = {k: v for k, v in _L0_gnn_all.items() if k in ('mlp1_w', 'mlp1_b', 'mlp2_w', 'mlp2_b', 'W_fc', 'a_fc', 'W_hand', 'a_hand')}
    del _L0_gnn_all

    def _L1_gnn_setup():
        import jax, jax.numpy as jnp
        import numpy as np
        B, N, D_IN, D_OUT, H = (64, 256, 128, 128, 4)
        HD = D_OUT // H
        key = jax.random.key(seed)
        ks = jax.random.split(key, 10)
        x = jax.random.normal(ks[0], (B, N, D_IN), dtype=jnp.float32)
        adj = jax.random.randint(ks[1], (N, N), 0, 2, dtype=jnp.int32)
        adj = adj.at[jnp.arange(N), jnp.arange(N)].set(1)
        s_in = 1.0 / np.sqrt(D_IN)
        s_out = 1.0 / np.sqrt(D_OUT)
        wq = jax.random.uniform(ks[2], (D_OUT, D_IN), jnp.float32, -s_in, s_in)
        bq = jax.random.uniform(ks[3], (D_OUT,), jnp.float32, -s_in, s_in)
        wk = jax.random.uniform(ks[4], (D_OUT, D_IN), jnp.float32, -s_in, s_in)
        bk = jax.random.uniform(ks[5], (D_OUT,), jnp.float32, -s_in, s_in)
        wv = jax.random.uniform(ks[6], (D_OUT, D_IN), jnp.float32, -s_in, s_in)
        bv = jax.random.uniform(ks[7], (D_OUT,), jnp.float32, -s_in, s_in)
        wo = jax.random.uniform(ks[8], (D_OUT, D_OUT), jnp.float32, -s_out, s_out)
        bo = jax.random.uniform(ks[9], (D_OUT,), jnp.float32, -s_out, s_out)
        return {'x': x, 'adj': adj, 'wq': wq, 'bq': bq, 'wk': wk, 'bk': bk, 'wv': wv, 'bv': bv, 'wo': wo, 'bo': bo}
    _L1_gnn_all = _L1_gnn_setup()
    _L1_gnn_in = {k: v for k, v in _L1_gnn_all.items() if k in ('wq', 'bq', 'wk', 'bk', 'wv', 'bv', 'wo', 'bo')}
    del _L1_gnn_all
    return {'x': x, 'adj': adj, 'L0_gnn_mlp1_w': _L0_gnn_in['mlp1_w'], 'L0_gnn_mlp1_b': _L0_gnn_in['mlp1_b'], 'L0_gnn_mlp2_w': _L0_gnn_in['mlp2_w'], 'L0_gnn_mlp2_b': _L0_gnn_in['mlp2_b'], 'L0_gnn_W_fc': _L0_gnn_in['W_fc'], 'L0_gnn_a_fc': _L0_gnn_in['a_fc'], 'L0_gnn_W_hand': _L0_gnn_in['W_hand'], 'L0_gnn_a_hand': _L0_gnn_in['a_hand'], 'L1_gnn_wq': _L1_gnn_in['wq'], 'L1_gnn_bq': _L1_gnn_in['bq'], 'L1_gnn_wk': _L1_gnn_in['wk'], 'L1_gnn_bk': _L1_gnn_in['bk'], 'L1_gnn_wv': _L1_gnn_in['wv'], 'L1_gnn_bv': _L1_gnn_in['bv'], 'L1_gnn_wo': _L1_gnn_in['wo'], 'L1_gnn_bo': _L1_gnn_in['bo']}

def reference(x, adj, L0_gnn_mlp1_w, L0_gnn_mlp1_b, L0_gnn_mlp2_w, L0_gnn_mlp2_b, L0_gnn_W_fc, L0_gnn_a_fc, L0_gnn_W_hand, L0_gnn_a_hand, L1_gnn_wq, L1_gnn_bq, L1_gnn_wk, L1_gnn_bk, L1_gnn_wv, L1_gnn_bv, L1_gnn_wo, L1_gnn_bo):
    import jax
    import jax.numpy as jnp

    def _L0_gnn_ref(x, adj, mlp1_w, mlp1_b, mlp2_w, mlp2_b, W_fc, a_fc, W_hand, a_hand):
        import jax, jax.numpy as jnp
        import numpy as np
        ALPHA = 0.2
        NEG_INF = -9000000000000000.0

        def _gat(inp, adj_mask, W, a):
            h = jnp.matmul(inp, W)
            F_ = h.shape[-1]
            f1 = jnp.matmul(h, a[:F_, 0])
            f2 = jnp.matmul(h, a[F_:, 0])
            e = jax.nn.leaky_relu(f1[:, :, None] + f2[:, None, :], ALPHA)
            if adj_mask is not None:
                e = jnp.where(adj_mask[None, :, :] > 0, e, NEG_INF)
            att = jax.nn.softmax(e, axis=2)
            h_prime = jnp.einsum('bij,bjf->bif', att, h)
            return jax.nn.elu(h_prime)
        out = jax.nn.relu(jnp.matmul(x, mlp1_w) + mlp1_b)
        residual = out
        out = _gat(jax.nn.relu(out), None, W_fc, a_fc)
        out = jax.nn.elu(out) + residual
        out = jax.nn.relu(jnp.matmul(out, mlp2_w) + mlp2_b)
        residual = out
        out = _gat(jax.nn.relu(out), adj, W_hand, a_hand)
        out = jax.nn.elu(out) + residual
        return jax.nn.relu(out)

    def _L1_gnn_ref(x, adj, wq, bq, wk, bk, wv, bv, wo, bo):
        import jax, jax.numpy as jnp
        import numpy as np
        B, N, D_IN, D_OUT, H = (64, 256, 128, 128, 4)
        HD = D_OUT // H
        b, n, _ = x.shape
        q = (x @ wq.T + bq).reshape(b, n, H, HD).transpose(0, 2, 1, 3)
        k = (x @ wk.T + bk).reshape(b, n, H, HD).transpose(0, 2, 1, 3)
        v = (x @ wv.T + bv).reshape(b, n, H, HD).transpose(0, 2, 1, 3)
        scores = jnp.einsum('bhnd,bhmd->bhnm', q, k) / jnp.sqrt(jnp.float32(HD))
        scores = jnp.where(adj[None, None] == 0, -jnp.inf, scores)
        attn = jnp.nan_to_num(jax.nn.softmax(scores, axis=-1), nan=0.0)
        out = jnp.einsum('bhnm,bhmd->bhnd', attn, v)
        out = out.transpose(0, 2, 1, 3).reshape(b, n, D_OUT)
        return out @ wo.T + bo
    x = _layernorm(x + _L0_gnn_ref(x, adj, L0_gnn_mlp1_w, L0_gnn_mlp1_b, L0_gnn_mlp2_w, L0_gnn_mlp2_b, L0_gnn_W_fc, L0_gnn_a_fc, L0_gnn_W_hand, L0_gnn_a_hand), axis=-1)
    x = _layernorm(x + _L1_gnn_ref(x, adj, L1_gnn_wq, L1_gnn_bq, L1_gnn_wk, L1_gnn_bk, L1_gnn_wv, L1_gnn_bv, L1_gnn_wo, L1_gnn_bo), axis=-1)
    return x

_drawn_inputs = setup_inputs


def setup_inputs(seed=0):
    import zlib

    import numpy as np

    out = dict(_drawn_inputs(seed))
    spreads = {'L0_gnn_mlp1_b': (0.0, 0.1), 'L0_gnn_mlp2_b': (0.0, 0.1)}
    factors = {'L1_gnn_wq': 5.177, 'L1_gnn_bq': 8.0, 'L1_gnn_wk': 5.319, 'L1_gnn_bk': 8.0}
    for name, (base, spread) in spreads.items():
        noise = np.random.default_rng([zlib.crc32(name.encode()), seed]).standard_normal(out[name].shape)
        drawn = base * np.exp(spread * noise) if base else spread * noise
        out[name] = jnp.asarray(drawn.astype(out[name].dtype))
    for name, factor in factors.items():
        out[name] = (out[name] * factor).astype(out[name].dtype)
    return out
```

```python
from contextlib import ExitStack

import concourse.bass as bass
from concourse import mybir

ALU = mybir.AluOpType
ACT = mybir.ActivationFunctionType
AX = mybir.AxisListType
F32 = mybir.dt.float32
F16 = mybir.dt.float16
BF16 = mybir.dt.bfloat16
I32 = mybir.dt.int32

P = 128
BANK = 512
ALPHA = 0.2
R_TOP = 75.0
MASKED = -1.0e30
GAT_ONLY = -(2.0 ** -100)
M_TOP = 60000.0
TINY = 1.0e-30
EPS = 1.0e-5


class Signal:

    def __init__(self, ctx, nc, name, per, first=0):
        self.sem, self.per, self.first = ctx.enter_context(nc.semaphore(name)), per, first

    def at(self, b, n):
        return b * self.per + (n + self.first)


class Fills:

    def __init__(self, order):
        self.first, self.reader, self.nth = {}, [], []
        for name, count, reader in order:
            self.first[name] = len(self.reader)
            for _ in range(count):
                self.nth.append(self.reader.count(reader))
                self.reader.append(reader)
        self.total = len(self.reader)

    def index(self, name, k=0):
        return self.first[name] + k

    def emptied(self, n):
        return self.nth[n] + 1

    def count(self, reader):
        return self.reader.count(reader)


def build(nc, x, adj, w1, b1, w2, b2, wfc, wfcT, afc, wh, whT, ah, wqT, bq, wkT, bk, wvT, bv, woT, bo, eye, out):
    B, N, D = x.shape
    NT = N // P
    NC = N // BANK
    TC = BANK // P
    F = w1.shape[1]
    FK = F // P
    H = 4
    HD = D // H
    GW = F + 1
    HW = D + 1
    SCALE = float(HD) ** -0.5
    KS = 3 * HD
    assert D == P and FK == 2 and NC == 2

    XF = Fills([("xT", NC, "act"), ("r1", FK * NC, "act"), ("h", NT, "act"), ("top1", 1, "dve"),
                ("f1", NC, "dve"), ("att1", NT, "dve"), ("zT", FK * NC, "dve"), ("r2", NC, "act"),
                ("h2", NT // 2, "act"), ("top2", 1, "dve"), ("f12", NC, "dve"), ("hm", 1, "dve"),
                ("att2", NT // 2, "dve"), ("r2n", NC, "dve"), ("x1T", NC, "act")])
    SF = Fills([("q", 1, "dve"), ("k", 1, "dve"), ("v", 1, "dve"), ("max", H * NT, "dve"),
                ("st", NC * NT * 2, "act"), ("on", 1, "dve"), ("onT", 1, "act"), ("proj", 1, "dve")])

    with ExitStack() as ctx:
        def sb(name, shape, dt=F32):
            return ctx.enter_context(nc.sbuf_tensor(name, shape, dt))

        def ps(name, shape, dt=F32):
            return ctx.enter_context(nc.psum_tensor(name, shape, dt))

        def signal(name, per=1, first=0):
            return Signal(ctx, nc, name, per, first)

        ident = sb("ident", [P, P])
        identb = sb("identb", [P, P], BF16)
        ones = sb("ones", [P, P])
        headsel = sb("headsel", [P, H])
        w1s = sb("w1s", [P, F])
        w2s = sb("w2s", [P, FK, D])
        wfx = sb("wfx", [P, FK, GW])
        wfTs = sb("wfTs", [P, FK, F])
        wa1 = sb("wa1", [P, FK, P])
        whx = sb("whx", [P, HW])
        whTs = sb("whTs", [P, D])
        wh1 = sb("wh1", [P, P])
        afs = sb("afs", [P, FK, 2])
        ahs = sb("ahs", [P, 2])
        b1s = sb("b1s", [P, FK])
        b2s = sb("b2s", [P, 1])
        wqs, wks, wvs, wos = (sb(n, [P, D]) for n in ("wqs", "wks", "wvs", "wos"))
        bqs, bks = sb("bqs", [P, 1]), sb("bks", [P, 1])
        bvs, bos = sb("bvs", [P, D]), sb("bos", [P, D])
        mask = sb("mask", [P, NT, N], BF16)
        maskT = sb("maskT", [P, NT, N], BF16)
        neg = sb("neg", [P, N], BF16)
        rowtop = sb("rowtop", [P, NT])
        dead = sb("dead", [P, NT])
        half = sb("half", [P, NT])
        minus1 = sb("minus1", [P, 1])
        xin = sb("xin", [P, NT, D])
        xT = sb("xT", [P, N])
        r1T = sb("r1T", [P, FK, N])
        hx = sb("hx", [P, NT, GW + 1])
        r2T = sb("r2T", [P, N])
        r2sum = sb("r2sum", [P, NC])
        h2x = sb("h2x", [P, NT, HW + 1])
        r2bc = sb("r2bc", [P, P])
        hmean = sb("hmean", [P, D])
        f2top = sb("f2top", [P, 1])
        diag = sb("diag", [P, P])
        top = sb("top", [P, 3])
        uv = sb("uv", [P, 2, NT])
        rrep = sb("rrep", [P, N])
        pw = sb("pw", [P, NT, N])

        rden = sb("rden", [P, NT])
        att = sb("att", [P, NT, F])
        el = sb("el", [P, NT, F])
        stat = sb("stat", [P, 8, NT])
        x1 = sb("x1", [P, NT, D])
        x1T = sb("x1T", [P, N])
        qkhi = sb("qkhi", [P, 2, N], F16)
        qklo = sb("qklo", [P, 2, N], F16)
        qst = sb("qst", [KS + 1, H, N], F16)
        kst = sb("kst", [KS + 1, H, N], F16)
        vs = sb("vs", [P, NT, D])
        junk = sb("junk", [P, N], BF16)
        mx = sb("mx", [P, H * NT])
        mrow = sb("mrow", [H * NT, P], F16)
        pt = sb("pt", [P, 2, H, BANK])
        oT = sb("oT", [P, N])
        dT = sb("dT", [P, N])
        sq2 = dT[:, :].rearrange("p (t d) -> p t d", d=D)
        dn = sb("dn", [P, NT, H])
        on = sb("on", [P, NT, D])
        y2 = sb("y2", [P, NT, D])
        stat2 = sb("stat2", [P, 8, NT])
        px = [ps(f"px{n}", [P, BANK]) for n in range(2)]
        pss = [ps(f"pss{n}", [P, N]) for n in range(2)]
        po = ps("po", [P, BANK])
        pd = ps("pd", [P, BANK])

        s_w = signal("s_w")
        s_adj = signal("s_adj")
        s_const = signal("s_const")
        s_neg = signal("s_neg")
        s_mask = signal("s_mask")
        s_dead = signal("s_dead")
        s_mtr = signal("s_mtr")
        s_mtc = signal("s_mtc")
        s_wa = signal("s_wa")
        s_wac = signal("s_wac")
        s_xin = signal("s_xin", 16)
        x_full = signal("x_full", XF.total)
        x_act = signal("x_act", XF.count("act"), 1)
        x_dve = signal("x_dve", XF.count("dve"), 1)
        s_f2top = signal("s_f2top", 2)
        s_diag = signal("s_diag", 2)
        s_topn = signal("s_topn", 4)
        s_uv = signal("s_uv", 4)
        s_r = signal("s_r", 2 * NC)
        s_p1 = signal("s_p1", NT)
        s_p2 = signal("s_p2", 2 * NT)
        s_rden = signal("s_rden", NT)
        s_min = signal("s_min", 3)
        s_e1 = signal("s_e1", 3)
        s_e2 = signal("s_e2", 3)
        s_z = signal("s_z", 3)
        s_bc = signal("s_bc", 2)
        s_den2 = signal("s_den2", 2 * (NT // 2))
        s_x2 = signal("s_x2", NT)
        s_y = signal("s_y", NC, 1)
        s_ln = signal("s_ln", 10)
        s_sq = signal("s_sq", 1)
        s_pow = signal("s_pow", 1)
        s_full = signal("s_full", SF.total)
        f_act = signal("f_act", SF.count("act"), 1)
        f_dve = signal("f_dve", SF.count("dve"), 1)
        s_hi = signal("s_hi", 2)
        s_stq = signal("s_stq", 16 * 3 * H)
        s_stk = signal("s_stk", 16 * 3 * H)
        s_go = signal("s_go", H * NT)
        s_mxT = signal("s_mxT", 1)
        s_mrow = signal("s_mrow", 1)
        s_mdma = signal("s_mdma", 16)
        s_pv = signal("s_pv", NC * NT, 1)
        s_oT = signal("s_oT", 2 * NC)
        s_dn = signal("s_dn", 1)
        s_dnr = signal("s_dnr", 2)
        s_y2 = signal("s_y2", 1)
        s_ln2 = signal("s_ln2", 10)
        s_sq2 = signal("s_sq2", 1)
        s_pow2 = signal("s_pow2", 1)
        s_out = signal("s_out", 16, 1)

        x_nat = x.rearrange("b (t p) d -> b p t d", p=P)
        o_nat = out.rearrange("b (t p) d -> b p t d", p=P)
        N_W = 18
        CONSTS = 7

        block = ctx.enter_context(nc.Block())

        @block.sync
        def _(sp):
            sp.sem_inc(s_out.sem, 1)
            sp.dma_start(pw[:, :, :].bitcast(I32), adj.rearrange("(t p) j -> p t j", p=P)).then_inc(s_adj.sem, 16)
            for dst, src in (
                (ident[:, :], eye), (w1s[:, :], w1), (b1s[:, :], b1),
                (wfx[:, :, 1:GW], wfc.rearrange("(k p) f -> p k f", p=P)),
                (wfTs[:, :, :], wfcT.rearrange("(k p) f -> p k f", p=P)),
                (afs[:, :, :], afc),
                (w2s[:, :, :], w2.rearrange("(k p) f -> p k f", p=P)),
                (b2s[:, :], b2.rearrange("(p o) -> p o", o=1)),
                (whx[:, 1:HW], wh), (whTs[:, :], whT),
                (ahs[:, :], ah),
                (wqs[:, :], wqT), (wks[:, :], wkT), (wvs[:, :], wvT), (wos[:, :], woT),
                (bqs[:, :], bq.rearrange("(p o) -> p o", o=1)), (bks[:, :], bk.rearrange("(p o) -> p o", o=1)),
                (bvs[:, :], bv), (bos[:, :], bo),
            ):
                sp.dma_start(dst, src).then_inc(s_w.sem, 16)
            with sp.Fori(0, B) as b:
                sp.wait_ge(s_y.sem, s_y.at(b, 0))
                sp.dma_start(xin[:, :, :], x_nat[b]).then_inc(s_xin.sem, 16)
                for n, (st, parts, sig) in enumerate(((qst, (qkhi, qklo, qkhi), s_stq),
                                                      (kst, (qkhi, qkhi, qklo), s_stk))):
                    sp.wait_ge(f_dve.sem, f_dve.at(b, n + 1))
                    for g, part in enumerate(parts):
                        for h in range(H):
                            sp.dma_start(st[g * HD:(g + 1) * HD, h, :],
                                         part[h * HD:(h + 1) * HD, n, :]).then_inc(sig.sem, 16)
                sp.wait_ge(s_mrow.sem, s_mrow.at(b, 1))
                sp.dma_start(qst[KS:KS + 1, :, :].rearrange("o h (t c) -> o (h t) c", c=P),
                             mrow[:, :]).then_inc(s_mdma.sem, 16)
                sp.wait_ge(s_ln2.sem, s_ln2.at(b, 10))
                sp.dma_start(o_nat[b], y2[:, :, :]).then_inc(s_out.sem, 16)
            sp.wait_ge(s_out.sem, 16 * B + 1)

        @block.gpsimd
        def _(pool):
            for n, (dst, value) in enumerate(((ones[:, :], 1.0), (hx[:, :, GW:GW + 1], 1.0), (h2x[:, :, HW:HW + 1], 1.0),
                                              (kst[KS:KS + 1, :, :], -1.0), (half[:, :], -0.5))):
                nc.gpsimd.memset(dst, value).then_inc(s_const.sem, 1)
                pool.wait_ge(s_const.sem, n + 1)
            pool.wait_ge(s_w.sem, 16 * (N_W + 1))
            nc.gpsimd.tensor_copy(headsel[:, :], ident[:, 0:P:HD]).then_inc(s_const.sem, 1)
            pool.wait_ge(s_const.sem, CONSTS - 1)
            nc.gpsimd.tensor_copy(identb[:, :], ident[:, :]).then_inc(s_const.sem, 1)
            pool.wait_ge(s_const.sem, CONSTS)
            with pool.Fori(0, B) as b:
                for st, ln, done in ((stat, s_ln, s_pow), (stat2, s_ln2, s_pow2)):
                    pool.wait_ge(ln.sem, ln.at(b, 5))
                    nc.gpsimd.tensor_tensor(st[:, 3, :], st[:, 2, :], half[:, :], ALU.pow).then_inc(done.sem, 1)

        @block.scalar
        def _(act):
            act.sem_inc(x_act.sem, 1)
            act.sem_inc(f_act.sem, 1)
            for jt in range(NT):
                act.wait_ge(s_mtr.sem, jt + 1)
                nc.scalar.activation(maskT[:, jt, :], px[jt % 2][:, :].bitcast(BF16), ACT.Copy).then_inc(s_mtc.sem, 1)

            def x_filled(b, name, k=0):
                act.wait_ge(x_full.sem, x_full.at(b, XF.index(name, k) + 1))

            def elus(b, n, part):
                act.wait_ge(s_min.sem, s_min.at(b, n + 1))
                nc.scalar.activation(part, part, ACT.Exp).then_inc(s_e1.sem, 1)
                act.wait_ge(s_e1.sem, s_e1.at(b, n + 1))
                nc.scalar.activation(part, part, ACT.Exp, bias=minus1[:, :]).then_inc(s_e2.sem, 1)

            def weights(b, n, hxt):
                act.wait_ge(s_topn.sem, s_topn.at(b, 2 * n + 2))
                if n == 1:
                    act.wait_ge(s_p1.sem, s_p1.at(b, NT))
                nc.scalar.activation(uv[:, 0, :], hxt[:, :, 0], ACT.Exp, bias=top[:, 1:2]).then_inc(s_uv.sem, 1)
                nc.scalar.activation(uv[:, 1, :], hxt[:, :, 0], ACT.Exp, bias=top[:, 2:3],
                                     scale=ALPHA).then_inc(s_uv.sem, 1)
                for c in range(NC):
                    k = XF.emptied(XF.index(("f1", "f12")[n], c))
                    act.wait_ge(x_dve.sem, x_dve.at(b, k))
                    nc.scalar.activation(rrep[:, c * BANK:(c + 1) * BANK], rrep[:, c * BANK:(c + 1) * BANK],
                                         ACT.Exp, scale=1.0 - ALPHA).then_inc(s_r.sem, 1)


            act.wait_ge(s_w.sem, 16 * (N_W + 1))
            act.wait_ge(s_const.sem, CONSTS)
            act.wait_ge(s_wac.sem, 4)
            with act.Fori(0, B) as b:
                for c in range(NC):
                    x_filled(b, "xT", c)
                    nc.scalar.activation(xT[:, c * BANK:(c + 1) * BANK], px[XF.index("xT", c) % 2][:, :],
                                         ACT.Copy).then_inc(x_act.sem, 1)
                for k in range(FK):
                    for c in range(NC):
                        n = k * NC + c
                        x_filled(b, "r1", n)
                        nc.scalar.activation(r1T[:, k, c * BANK:(c + 1) * BANK], px[XF.index("r1", n) % 2][:, :],
                                             ACT.Relu, bias=b1s[:, k:k + 1]).then_inc(x_act.sem, 1)
                for jt in range(NT):
                    x_filled(b, "h", jt)
                    nc.scalar.activation(hx[:, jt, 0:GW], px[XF.index("h", jt) % 2][:, 0:GW],
                                         ACT.Copy).then_inc(x_act.sem, 1)
                weights(b, 0, hx)
                for n in range(2):
                    elus(b, n, el[:, n * NT // 2:(n + 1) * NT // 2, :])
                for c in range(NC):
                    x_filled(b, "r2", c)
                    nc.scalar.activation(r2T[:, c * BANK:(c + 1) * BANK], px[XF.index("r2", c) % 2][:, :],
                                         ACT.Relu, bias=b2s[:, :],
                                         accum_out=r2sum[:, c:c + 1]).then_inc(x_act.sem, 1)
                for n in range(NT // 2):
                    x_filled(b, "h2", n)
                    nc.scalar.activation(h2x[:, 2 * n:2 * n + 2, 0:HW],
                                         px[XF.index("h2", n) % 2][:, 0:2 * HW].rearrange("p (t f) -> p t f", t=2),
                                         ACT.Copy).then_inc(x_act.sem, 1)
                weights(b, 1, h2x)
                elus(b, 2, el[:, 0:NT // 2, :])
                act.wait_ge(s_ln.sem, s_ln.at(b, 3))
                nc.scalar.activation(el[:, 0:NT // 2, :].rearrange("p t f -> p (t f)"),
                                     att[:, NT // 2:NT, :].rearrange("p t f -> p (t f)"),
                                     ACT.Square).then_inc(s_sq.sem, 1)
                for c in range(NC):
                    x_filled(b, "x1T", c)
                    nc.scalar.activation(x1T[:, c * BANK:(c + 1) * BANK], px[XF.index("x1T", c) % 2][:, :],
                                         ACT.Copy).then_inc(x_act.sem, 1)
                for n, bias in enumerate((bqs, bks)):
                    act.wait_ge(s_full.sem, s_full.at(b, SF.index("q", n) + 1))
                    nc.scalar.activation(qkhi[:, n, :], pss[n % 2][:, :], ACT.Identity,
                                         bias=bias[:, :]).then_inc(s_hi.sem, 1)
                for c in range(NC):
                    for jt in range(NT):
                        for hp in range(2):
                            n = (c * NT + jt) * 2 + hp
                            if c * NT + jt >= 2:
                                act.wait_ge(s_pv.sem, s_pv.at(b, c * NT + jt - 1))
                            else:
                                act.wait_ge(s_pv.sem, s_pv.at(b, 0))
                            act.wait_ge(s_full.sem, s_full.at(b, SF.index("st", n) + 1))
                            nc.scalar.activation(
                                pt[:, jt % 2, 2 * hp:2 * hp + 2, :].rearrange("p h c -> p (h c)"),
                                pss[SF.index("st", n) % 2][:, :], ACT.Exp, scale=SCALE).then_inc(f_act.sem, 1)
                act.wait_ge(s_full.sem, s_full.at(b, SF.index("onT") + 1))
                nc.scalar.activation(oT[:, :], pss[SF.index("onT") % 2][:, :], ACT.Copy).then_inc(f_act.sem, 1)
                act.wait_ge(s_ln2.sem, s_ln2.at(b, 3))
                nc.scalar.activation(dT[:, :],
                                     on[:, :, :].rearrange("p t f -> p (t f)"), ACT.Square).then_inc(s_sq2.sem, 1)

        @block.vector
        def _(dve):
            dve.sem_inc(x_dve.sem, 1)
            dve.sem_inc(f_dve.sem, 1)
            dve.sem_inc(s_y.sem, 1)
            nc.vector.memset(minus1[:, :], -1.0).then_inc(s_dead.sem, 1)
            dve.wait_ge(s_adj.sem, 16)
            for it in range(NT):
                a = pw[:, it, :].bitcast(I32)
                if it:
                    dve.wait_ge(s_mask.sem, 2 * it)
                nc.vector.tensor_scalar(neg[:, :], a, 0, GAT_ONLY, ALU.is_lt, ALU.mult).then_inc(s_neg.sem, 1)
                nc.vector.tensor_scalar(mask[:, it, :], a, 0, MASKED, ALU.is_equal, ALU.mult).then_inc(s_mask.sem, 1)
                dve.wait_ge(s_neg.sem, it + 1)
                dve.wait_ge(s_mask.sem, 2 * it + 1)
                nc.vector.tensor_tensor(mask[:, it, :], mask[:, it, :], neg[:, :], ALU.add).then_inc(s_mask.sem, 1)
            for it in range(NT):
                dve.wait_ge(s_mask.sem, 2 * it + 2)
                nc.vector.reduce_max(rowtop[:, it:it + 1], mask[:, it, :], axis=AX.X).then_inc(s_dead.sem, 1)
            dve.wait_ge(s_dead.sem, NT + 1)
            nc.vector.tensor_scalar(dead[:, :], rowtop[:, :], 0.0, None, ALU.is_lt).then_inc(s_dead.sem, 1)
            dve.wait_ge(s_wa.sem, FK + 1)
            for k in range(FK):
                nc.vector.tensor_copy(wfx[:, k, 0:1], po[:, 2 * k + 1:2 * k + 2]).then_inc(s_wac.sem, 1)
                nc.vector.tensor_scalar(wa1[:, k, :], ones[:, :], po[:, 2 * k:2 * k + 1], None,
                                        ALU.mult).then_inc(s_dead.sem, 1)
            nc.vector.tensor_copy(whx[:, 0:1], po[:, 5:6]).then_inc(s_wac.sem, 1)
            nc.vector.tensor_scalar(wh1[:, :], ones[:, :], po[:, 4:5], None, ALU.mult).then_inc(s_wac.sem, 1)

            def x_filled(b, name, k=0):
                dve.wait_ge(x_full.sem, x_full.at(b, XF.index(name, k) + 1))
                return px[XF.index(name, k) % 2]

            def find_top(b, n, hxt):
                done = XF.emptied(XF.index(("h", "h2")[n], (NT, NT // 2)[n] - 1))
                dve.wait_ge(x_act.sem, x_act.at(b, done))
                nc.vector.reduce_max(f2top[:, :], hxt[:, :, 0], axis=AX.X).then_inc(s_f2top.sem, 1)
                dve.wait_ge(s_f2top.sem, s_f2top.at(b, n + 1))
                nc.vector.tensor_scalar(diag[:, :], ident[:, :], f2top[:, :], None, ALU.mult).then_inc(s_diag.sem, 1)
                src = x_filled(b, ("top1", "top2")[n])
                nc.vector.reduce_max(top[:, 0:1], src[:, 0:P], axis=AX.X).then_inc(x_dve.sem, 1)
                dve.wait_ge(x_dve.sem, x_dve.at(b, XF.emptied(XF.index(("top1", "top2")[n]))))
                nc.vector.tensor_scalar(top[:, 1:2], top[:, 0:1], -1.0, None, ALU.mult).then_inc(s_topn.sem, 1)
                nc.vector.tensor_scalar(top[:, 2:3], top[:, 0:1], -ALPHA, None, ALU.mult).then_inc(s_topn.sem, 1)
                for c in range(NC):
                    src = x_filled(b, ("f1", "f12")[n], c)
                    nc.vector.tensor_scalar(rrep[:, c * BANK:(c + 1) * BANK], src[:, :], top[:, 0:1], R_TOP,
                                            ALU.add, ALU.min).then_inc(x_dve.sem, 1)
                dve.wait_ge(s_uv.sem, s_uv.at(b, 2 * n + 2))
                dve.wait_ge(s_r.sem, s_r.at(b, NC * (n + 1)))

            def layer_norm(b, ln, sq_done, pow_done, y, yc, sq, st, res):
                def bc(row):
                    return st[:, row, :].unsqueeze(2).to_broadcast([P, NT, D])
                nc.vector.reduce_sum(st[:, 0, :], y, axis=AX.X).then_inc(ln.sem, 1)
                dve.wait_ge(ln.sem, ln.at(b, 1))
                nc.vector.tensor_scalar(st[:, 1, :], st[:, 0, :], 1.0 / D, None, ALU.mult).then_inc(ln.sem, 1)
                dve.wait_ge(ln.sem, ln.at(b, 2))
                nc.vector.tensor_tensor(yc, y, bc(1), ALU.subtract).then_inc(ln.sem, 1)
                dve.wait_ge(sq_done.sem, sq_done.at(b, 1))
                nc.vector.reduce_sum(st[:, 0, :], sq, axis=AX.X).then_inc(ln.sem, 1)
                dve.wait_ge(ln.sem, ln.at(b, 4))
                nc.vector.tensor_scalar(st[:, 2, :], st[:, 0, :], 1.0 / D, EPS, ALU.mult, ALU.add).then_inc(ln.sem, 1)
                dve.wait_ge(pow_done.sem, pow_done.at(b, 1))
                nc.vector.tensor_tensor(st[:, 4, :], st[:, 3, :], st[:, 3, :], ALU.mult).then_inc(ln.sem, 1)
                dve.wait_ge(ln.sem, ln.at(b, 6))
                nc.vector.tensor_tensor(st[:, 5, :], st[:, 4, :], st[:, 2, :], ALU.mult).then_inc(ln.sem, 1)
                dve.wait_ge(ln.sem, ln.at(b, 7))
                nc.vector.tensor_scalar(st[:, 6, :], st[:, 5, :], -0.5, 1.5, ALU.mult, ALU.add).then_inc(ln.sem, 1)
                dve.wait_ge(ln.sem, ln.at(b, 8))
                nc.vector.tensor_tensor(st[:, 7, :], st[:, 3, :], st[:, 6, :], ALU.mult).then_inc(ln.sem, 1)
                dve.wait_ge(ln.sem, ln.at(b, 9))
                nc.vector.tensor_tensor(res, yc, bc(7), ALU.mult).then_inc(ln.sem, 1)

            dve.wait_ge(s_w.sem, 16 * (N_W + 1))
            dve.wait_ge(s_const.sem, CONSTS)
            dve.wait_ge(s_dead.sem, NT + 2 + FK)
            with dve.Fori(0, B) as b:
                find_top(b, 0, hx)
                for jt in range(NT):
                    if jt == 0:
                        dve.wait_ge(x_full.sem, x_full.at(b, XF.index("f1") + 1))
                    nc.vector.tensor_scalar(pw[:, jt, :], rrep[:, :], uv[:, 0, jt:jt + 1], uv[:, 1, jt:jt + 1],
                                            ALU.mult, ALU.max).then_inc(s_p1.sem, 1)
                for it in range(NT):
                    src = x_filled(b, "att1", it)
                    nc.vector.reciprocal(rden[:, it:it + 1], src[:, F:F + 1]).then_inc(s_rden.sem, 1)
                    dve.wait_ge(s_rden.sem, s_rden.at(b, it + 1))
                    nc.vector.tensor_scalar(att[:, it, :], src[:, 0:F], rden[:, it:it + 1], None,
                                            ALU.mult).then_inc(x_dve.sem, 1)
                    if it % (NT // 2) == NT // 2 - 1:
                        g = it // (NT // 2)
                        part = slice(g * NT // 2, (g + 1) * NT // 2)
                        dve.wait_ge(x_dve.sem, x_dve.at(b, XF.emptied(XF.index("att1", it))))
                        nc.vector.tensor_scalar(el[:, part, :], att[:, part, :], 0.0, None,
                                                ALU.min).then_inc(s_min.sem, 1)
                for g in range(2):
                    part = slice(g * NT // 2, (g + 1) * NT // 2)
                    dve.wait_ge(s_e2.sem, s_e2.at(b, g + 1))
                    nc.vector.scalar_tensor_tensor(
                        att[:, part, :].rearrange("p t f -> p (t f)"),
                        att[:, part, :].rearrange("p t f -> p (t f)"), 0.0,
                        el[:, part, :].rearrange("p t f -> p (t f)"), ALU.max, ALU.add).then_inc(s_z.sem, 1)
                for n in range(FK * NC):
                    k, c = n % FK, n // FK
                    src = x_filled(b, "zT", n)
                    r = r1T[:, k, c * BANK:(c + 1) * BANK]
                    nc.vector.scalar_tensor_tensor(r, src[:, :], -1.0, r, ALU.add, ALU.add).then_inc(x_dve.sem, 1)
                find_top(b, 1, h2x)
                nc.vector.tensor_tensor(r2sum[:, 0:1], r2sum[:, 0:1], r2sum[:, 1:2], ALU.add).then_inc(s_bc.sem, 1)
                dve.wait_ge(s_bc.sem, s_bc.at(b, 1))
                nc.vector.tensor_scalar(r2bc[:, :], ones[:, :], r2sum[:, 0:1], 1.0 / N, ALU.mult,
                                        ALU.mult).then_inc(s_bc.sem, 1)
                src = x_filled(b, "hm")
                nc.vector.tensor_copy(hmean[:, :], src[:, 0:D]).then_inc(x_dve.sem, 1)
                for jt in range(NT):
                    nc.vector.tensor_scalar(pw[:, jt, :], rrep[:, :], uv[:, 0, jt:jt + 1], uv[:, 1, jt:jt + 1],
                                            ALU.mult, ALU.max).then_inc(s_p2.sem, 1)
                    dve.wait_ge(s_p2.sem, s_p2.at(b, 2 * jt + 1))
                    nc.vector.scalar_tensor_tensor(pw[:, jt, :], maskT[:, jt, :], 0.0, pw[:, jt, :],
                                                   ALU.is_ge, ALU.mult).then_inc(s_p2.sem, 1)
                x2 = att[:, 0:NT // 2, :].rearrange("p t f -> p (t f)").rearrange("p (t f) -> p t f", t=NT)
                e2 = el[:, 0:NT // 2, :].rearrange("p t f -> p (t f)").rearrange("p (t f) -> p t f", t=NT)
                yc = att[:, NT // 2:NT, :].rearrange("p t f -> p (t f)").rearrange("p (t f) -> p t f", t=NT)
                for n in range(NT // 2):
                    tt = slice(2 * n, 2 * n + 2)
                    src = x_filled(b, "att2", n)[:, 0:2 * HW].rearrange("p (t f) -> p t f", t=2)
                    nc.vector.tensor_scalar(rden[:, tt], src[:, :, D], TINY, None, ALU.max).then_inc(s_den2.sem, 1)
                    dve.wait_ge(s_den2.sem, s_den2.at(b, 2 * n + 1))
                    nc.vector.reciprocal(rden[:, tt], rden[:, tt]).then_inc(s_den2.sem, 1)
                    dve.wait_ge(s_den2.sem, s_den2.at(b, 2 * n + 2))
                    nc.vector.tensor_tensor(x2[:, tt, :], src[:, :, 0:D],
                                            rden[:, tt].unsqueeze(2).to_broadcast([P, 2, D]),
                                            ALU.mult).then_inc(x_dve.sem, 1)
                dve.wait_ge(x_dve.sem, x_dve.at(b, XF.emptied(XF.index("att2", NT // 2 - 1))))
                for it in range(NT):
                    nc.vector.scalar_tensor_tensor(x2[:, it, :], hmean[:, :], dead[:, it:it + 1], x2[:, it, :],
                                                   ALU.mult, ALU.add).then_inc(s_x2.sem, 1)
                dve.wait_ge(s_x2.sem, s_x2.at(b, NT))
                nc.vector.tensor_scalar(e2, x2, 0.0, None, ALU.min).then_inc(s_min.sem, 1)
                dve.wait_ge(s_e2.sem, s_e2.at(b, 3))
                nc.vector.scalar_tensor_tensor(x2, x2, 0.0, e2, ALU.max, ALU.add).then_inc(s_z.sem, 1)
                dve.wait_ge(s_z.sem, s_z.at(b, 3))
                for c in range(NC):
                    src = x_filled(b, "r2n", c)[:, :].rearrange("p (t f) -> p t f", f=D)
                    tt = slice(c * TC, (c + 1) * TC)
                    nc.vector.scalar_tensor_tensor(x2[:, tt, :], src, -1.0, x2[:, tt, :], ALU.add,
                                                   ALU.add).then_inc(x_dve.sem, 1)
                    dve.wait_ge(x_dve.sem, x_dve.at(b, XF.emptied(XF.index("r2n", c))))
                    nc.vector.scalar_tensor_tensor(x2[:, tt, :], x2[:, tt, :], 0.0, xin[:, tt, :], ALU.max,
                                                   ALU.add).then_inc(s_y.sem, 1)
                dve.wait_ge(s_y.sem, s_y.at(b, NC))
                layer_norm(b, s_ln, s_sq, s_pow, x2, yc, e2, stat, x1[:, :, :])
                for n, bias in enumerate((bqs, bks)):
                    dve.wait_ge(s_hi.sem, s_hi.at(b, n + 1))
                    nc.vector.scalar_tensor_tensor(qklo[:, n, :], pss[n % 2][:, :], bias[:, :], qkhi[:, n, :],
                                                   ALU.add, ALU.subtract).then_inc(f_dve.sem, 1)
                dve.wait_ge(s_full.sem, s_full.at(b, SF.index("v") + 1))
                nc.vector.tensor_tensor(vs[:, :, :], pss[SF.index("v") % 2][:, :].rearrange("p (t f) -> p t f", f=D),
                                        bvs[:, :].unsqueeze(1).to_broadcast([P, NT, D]),
                                        ALU.add).then_inc(f_dve.sem, 1)
                for n in range(H * NT):
                    m = SF.index("max", n)
                    dve.wait_ge(f_dve.sem, f_dve.at(b, SF.emptied(m) - 1))
                    dve.wait_ge(s_full.sem, s_full.at(b, m + 1))
                    dve.sem_inc(s_go.sem, 1)
                    nc.vector.tensor_tensor_reduce(out=junk[:, :], in0=pss[m % 2][:, :], in1=mask[:, n % NT, :],
                                                   scale=1.0, scalar=-3.0e38, op0=ALU.add, op1=ALU.max,
                                                   accum_out=mx[:, n:n + 1]).then_inc(f_dve.sem, 1)
                dve.wait_ge(s_mxT.sem, s_mxT.at(b, 1))
                nc.vector.tensor_scalar(mrow[:, :], po[0:H * NT, 0:P], -M_TOP, M_TOP, ALU.max,
                                        ALU.min).then_inc(s_mrow.sem, 1)
                for c in range(NC):
                    cc = slice(c * BANK, (c + 1) * BANK)
                    dve.wait_ge(s_pv.sem, s_pv.at(b, (c + 1) * NT))
                    nc.vector.tensor_copy(oT[:, cc], po[:, :]).then_inc(s_oT.sem, 1)
                    nc.vector.tensor_copy(dT[:, cc], pd[:, :]).then_inc(s_oT.sem, 1)
                dve.wait_ge(s_dn.sem, s_dn.at(b, 1))
                nc.vector.tensor_scalar(dn[:, :, :], pd[:, 0:NT * H].rearrange("p (t h) -> p t h", h=H), TINY, None,
                                        ALU.max).then_inc(s_dnr.sem, 1)
                dve.wait_ge(s_dnr.sem, s_dnr.at(b, 1))
                nc.vector.reciprocal(dn[:, :, :], dn[:, :, :]).then_inc(s_dnr.sem, 1)
                dve.wait_ge(s_dnr.sem, s_dnr.at(b, 2))
                dve.wait_ge(s_full.sem, s_full.at(b, SF.index("on") + 1))
                nc.vector.tensor_tensor(on[:, :, :].rearrange("p t (h d) -> p (t h) d", h=H),
                                        pss[SF.index("on") % 2][:, :].rearrange("p (g d) -> p g d", d=HD),
                                        dn[:, :, :].rearrange("p t h -> p (t h)").unsqueeze(2)
                                        .to_broadcast([P, NT * H, HD]), ALU.mult).then_inc(f_dve.sem, 1)
                dve.wait_ge(s_full.sem, s_full.at(b, SF.index("proj") + 1))
                dve.wait_ge(s_out.sem, s_out.at(b, 0))
                nc.vector.tensor_tensor(y2[:, :, :], pss[SF.index("proj") % 2][:, :].rearrange("p (t f) -> p t f", f=D),
                                        x1[:, :, :], ALU.add).then_inc(f_dve.sem, 1)
                dve.wait_ge(f_dve.sem, f_dve.at(b, SF.count("dve")))
                nc.vector.tensor_tensor(y2[:, :, :], y2[:, :, :], bos[:, :].unsqueeze(1).to_broadcast([P, NT, D]),
                                        ALU.add).then_inc(s_y2.sem, 1)
                dve.wait_ge(s_y2.sem, s_y2.at(b, 1))
                layer_norm(b, s_ln2, s_sq2, s_pow2, y2[:, :, :], on[:, :, :], sq2, stat2, y2[:, :, :])

        @block.tensor
        def _(pe):
            pe.sem_inc(s_pv.sem, 1)
            pe.wait_ge(s_w.sem, 16 * (N_W + 1))
            pe.wait_ge(s_const.sem, CONSTS)
            for k in range(FK):
                for f in range(FK):
                    last = nc.tensor.matmul(po[:, 2 * k:2 * k + 2], wfTs[:, f, k * P:(k + 1) * P], afs[:, f, :],
                                            start=(f == 0), stop=(f == FK - 1))
                last.then_inc(s_wa.sem, 1)
            nc.tensor.matmul(po[:, 4:6], whTs[:, :], ahs[:, :], start=True, stop=True).then_inc(s_wa.sem, 1)
            pe.wait_ge(s_mask.sem, 2 * NT)
            for jt in range(NT):
                if jt >= 2:
                    pe.wait_ge(s_mtc.sem, jt - 1)
                for it in range(NT):
                    last = nc.tensor.transpose(px[jt % 2][:, :].bitcast(BF16)[:, it * P:(it + 1) * P],
                                               mask[:, it, jt * P:(jt + 1) * P], identb[:, :])
                last.then_inc(s_mtr.sem, 1)
            pe.wait_ge(s_mtc.sem, NT)
            pe.wait_ge(s_wac.sem, 4)
            pe.wait_ge(s_dead.sem, NT + 2 + FK)

            def x_room(b, name, k=0):
                n = XF.index(name, k)
                if n < 2:
                    pe.wait_ge(x_act.sem, x_act.at(b, 0))
                elif XF.reader[n - 2] == "act":
                    pe.wait_ge(x_act.sem, x_act.at(b, XF.emptied(n - 2)))
                else:
                    pe.wait_ge(x_dve.sem, x_dve.at(b, XF.emptied(n - 2)))
                return px[n % 2]

            def s_room(b, name, k=0):
                n = SF.index(name, k)
                if n < 2:
                    pe.wait_ge(f_dve.sem, f_dve.at(b, 0))
                    pe.wait_ge(f_act.sem, f_act.at(b, 0))
                elif SF.reader[n - 2] == "act":
                    pe.wait_ge(f_act.sem, f_act.at(b, SF.emptied(n - 2)))
                else:
                    pe.wait_ge(f_dve.sem, f_dve.at(b, SF.emptied(n - 2)))
                return pss[n % 2]

            def emptied_act(b, name, k=0):
                pe.wait_ge(x_act.sem, x_act.at(b, XF.emptied(XF.index(name, k))))

            def top_and_f1(b, n, w, src):
                dst = x_room(b, ("top1", "top2")[n])
                pe.wait_ge(s_diag.sem, s_diag.at(b, n + 1))
                nc.tensor.matmul(dst[:, 0:P], ones[:, :], diag[:, :], start=True, stop=True).then_inc(x_full.sem, 1)
                for c in range(NC):
                    dst = x_room(b, ("f1", "f12")[n], c)
                    for k in range(len(w)):
                        last = nc.tensor.matmul(dst[:, :], w[k], src[k][:, c * BANK:(c + 1) * BANK],
                                                start=(k == 0), stop=(k == len(w) - 1))
                    last.then_inc(x_full.sem, 1)

            with pe.Fori(0, B) as b:
                pe.wait_ge(s_xin.sem, s_xin.at(b, 16))
                for c in range(NC):
                    dst = x_room(b, "xT", c)
                    for t in range(TC):
                        last = nc.tensor.transpose(dst[:, t * P:(t + 1) * P], xin[:, c * TC + t, :], ident[:, :])
                    last.then_inc(x_full.sem, 1)
                for k in range(FK):
                    for c in range(NC):
                        dst = x_room(b, "r1", k * NC + c)
                        emptied_act(b, "xT", c)
                        nc.tensor.matmul(dst[:, :], w1s[:, k * P:(k + 1) * P], xT[:, c * BANK:(c + 1) * BANK],
                                         start=True, stop=True).then_inc(x_full.sem, 1)
                emptied_act(b, "r1", FK * NC - 1)
                for jt in range(NT):
                    dst = x_room(b, "h", jt)
                    for k in range(FK):
                        last = nc.tensor.matmul(dst[:, 0:GW], r1T[:, k, jt * P:(jt + 1) * P], wfx[:, k, :],
                                                start=(k == 0), stop=(k == FK - 1))
                    last.then_inc(x_full.sem, 1)
                top_and_f1(b, 0, [wa1[:, k, :] for k in range(FK)], [r1T[:, k, :] for k in range(FK)])
                for it in range(NT):
                    dst = x_room(b, "att1", it)
                    for jt in range(NT):
                        if it == 0:
                            pe.wait_ge(s_p1.sem, s_p1.at(b, jt + 1))
                        last = nc.tensor.matmul(dst[:, 0:GW], pw[:, jt, it * P:(it + 1) * P], hx[:, jt, 1:GW + 1],
                                                start=(jt == 0), stop=(jt == NT - 1))
                    last.then_inc(x_full.sem, 1)
                for n in range(FK * NC):
                    k, c = n % FK, n // FK
                    dst = x_room(b, "zT", n)
                    pe.wait_ge(s_z.sem, s_z.at(b, c + 1))
                    for t in range(TC):
                        last = nc.tensor.transpose(dst[:, t * P:(t + 1) * P],
                                                   att[:, c * TC + t, k * P:(k + 1) * P], ident[:, :])
                    last.then_inc(x_full.sem, 1)
                for c in range(NC):
                    dst = x_room(b, "r2", c)
                    pe.wait_ge(x_dve.sem, x_dve.at(b, XF.emptied(XF.index("zT", FK * (c + 1) - 1))))
                    for k in range(FK):
                        last = nc.tensor.matmul(dst[:, :], w2s[:, k, :], r1T[:, k, c * BANK:(c + 1) * BANK],
                                                start=(k == 0), stop=(k == FK - 1))
                    last.then_inc(x_full.sem, 1)
                for n in range(NT // 2):
                    dst = x_room(b, "h2", n)
                    emptied_act(b, "r2", 2 * n // TC)
                    for t in range(2):
                        jt = 2 * n + t
                        last = nc.tensor.matmul(dst[:, t * HW:(t + 1) * HW], r2T[:, jt * P:(jt + 1) * P], whx[:, :],
                                                start=True, stop=True)
                    last.then_inc(x_full.sem, 1)
                top_and_f1(b, 1, [wh1[:, :]], [r2T[:, :]])
                dst = x_room(b, "hm")
                pe.wait_ge(s_bc.sem, s_bc.at(b, 2))
                nc.tensor.matmul(dst[:, 0:D], r2bc[:, :], whx[:, 1:HW], start=True, stop=True).then_inc(x_full.sem, 1)
                for n in range(NT // 2):
                    dst = x_room(b, "att2", n)
                    for t in range(2):
                        it = 2 * n + t
                        for jt in range(NT):
                            if it == 0:
                                pe.wait_ge(s_p2.sem, s_p2.at(b, 2 * jt + 2))
                            last = nc.tensor.matmul(dst[:, t * HW:(t + 1) * HW], pw[:, jt, it * P:(it + 1) * P],
                                                    h2x[:, jt, 1:HW + 1], start=(jt == 0), stop=(jt == NT - 1))
                    last.then_inc(x_full.sem, 1)
                for c in range(NC):
                    dst = x_room(b, "r2n", c)
                    for t in range(TC):
                        n = c * TC + t
                        last = nc.tensor.transpose(dst[:, t * P:(t + 1) * P], r2T[:, n * P:(n + 1) * P], ident[:, :])
                    last.then_inc(x_full.sem, 1)
                pe.wait_ge(s_ln.sem, s_ln.at(b, 10))
                for c in range(NC):
                    dst = x_room(b, "x1T", c)
                    for t in range(TC):
                        last = nc.tensor.transpose(dst[:, t * P:(t + 1) * P], x1[:, c * TC + t, :], ident[:, :])
                    last.then_inc(x_full.sem, 1)
                emptied_act(b, "x1T", NC - 1)
                for n, w in enumerate((wqs, wks)):
                    dst = s_room(b, "q", n)
                    for c in range(NC):
                        last = nc.tensor.matmul(dst[:, c * BANK:(c + 1) * BANK], w[:, :],
                                                x1T[:, c * BANK:(c + 1) * BANK], start=True, stop=True)
                    last.then_inc(s_full.sem, 1)
                dst = s_room(b, "v")
                for jt in range(NT):
                    last = nc.tensor.matmul(dst[:, jt * P:(jt + 1) * P], x1T[:, jt * P:(jt + 1) * P], wvs[:, :],
                                            start=True, stop=True)
                last.then_inc(s_full.sem, 1)
                pe.wait_ge(s_stq.sem, s_stq.at(b, 16 * 3 * H))
                pe.wait_ge(s_stk.sem, s_stk.at(b, 16 * 3 * H))
                for n in range(H * NT):
                    h, it = n // NT, n % NT
                    dst = s_room(b, "max", n)
                    for c in range(NC):
                        last = nc.tensor.matmul(dst[:, c * BANK:(c + 1) * BANK], qst[0:KS, h, it * P:(it + 1) * P],
                                                kst[0:KS, h, c * BANK:(c + 1) * BANK], start=True, stop=True)
                    last.then_inc(s_full.sem, 1)
                pe.wait_ge(f_dve.sem, f_dve.at(b, SF.emptied(SF.index("max", H * NT - 1))))
                nc.tensor.transpose(po[0:H * NT, 0:P], mx[:, :], ident[:, :]).then_inc(s_mxT.sem, 1)
                pe.wait_ge(s_mdma.sem, s_mdma.at(b, 16))

                def scores(c, jt):
                    for hp in range(2):
                        n = (c * NT + jt) * 2 + hp
                        dst = s_room(b, "st", n)
                        for g in range(2):
                            h = 2 * hp + g
                            nc.tensor.matmul(dst[:, g * BANK:(g + 1) * BANK], kst[:, h, jt * P:(jt + 1) * P],
                                             qst[:, h, c * BANK:(c + 1) * BANK], start=True, stop=False)
                            last = nc.tensor.matmul(dst[:, g * BANK:(g + 1) * BANK], identb[:, :],
                                                    maskT[:, jt, c * BANK:(c + 1) * BANK], start=False, stop=True)
                        last.then_inc(s_full.sem, 1)

                def products(c, jt):
                    n = (c * NT + jt) * 2 + 1
                    pe.wait_ge(f_act.sem, f_act.at(b, SF.emptied(SF.index("st", n))))
                    if c > 0 and jt == 0:
                        pe.wait_ge(s_oT.sem, s_oT.at(b, 2 * c))
                    for h in range(H):
                        nc.tensor.matmul(po[h * HD:(h + 1) * HD, :], vs[:, jt, h * HD:(h + 1) * HD],
                                         pt[:, jt % 2, h, :], start=(jt == 0), stop=(jt == NT - 1),
                                         tile_position=(0, h * HD))
                    for h in range(H):
                        last = nc.tensor.matmul(pd[h * HD:(h + 1) * HD, :], ones[:, 0:HD], pt[:, jt % 2, h, :],
                                                start=(jt == 0), stop=(jt == NT - 1), tile_position=(0, h * HD))
                    last.then_inc(s_pv.sem, 1)

                steps = [(c, jt) for c in range(NC) for jt in range(NT)]
                for n, (c, jt) in enumerate(steps):
                    scores(c, jt)
                    if n:
                        products(*steps[n - 1])
                products(*steps[-1])
                pe.wait_ge(s_oT.sem, s_oT.at(b, 2 * NC))
                for it in range(NT):
                    last = nc.tensor.matmul(pd[:, it * H:(it + 1) * H], dT[:, it * P:(it + 1) * P], headsel[:, :],
                                            start=True, stop=True)
                last.then_inc(s_dn.sem, 1)
                dst = s_room(b, "on")
                for it in range(NT):
                    last = nc.tensor.transpose(dst[:, it * P:(it + 1) * P], oT[:, it * P:(it + 1) * P], ident[:, :])
                last.then_inc(s_full.sem, 1)
                dst = s_room(b, "onT")
                pe.wait_ge(f_dve.sem, f_dve.at(b, SF.emptied(SF.index("on"))))
                for it in range(NT):
                    last = nc.tensor.transpose(dst[:, it * P:(it + 1) * P], on[:, it, :], ident[:, :])
                last.then_inc(s_full.sem, 1)
                dst = s_room(b, "proj")
                pe.wait_ge(f_act.sem, f_act.at(b, SF.emptied(SF.index("onT"))))
                for it in range(NT):
                    last = nc.tensor.matmul(dst[:, it * P:(it + 1) * P], oT[:, it * P:(it + 1) * P], wos[:, :],
                                            start=True, stop=True)
                last.then_inc(s_full.sem, 1)


def kernel(x, adj, L0_gnn_mlp1_w, L0_gnn_mlp1_b, L0_gnn_mlp2_w, L0_gnn_mlp2_b, L0_gnn_W_fc, L0_gnn_a_fc,
           L0_gnn_W_hand, L0_gnn_a_hand, L1_gnn_wq, L1_gnn_bq, L1_gnn_wk, L1_gnn_bk, L1_gnn_wv, L1_gnn_bv,
           L1_gnn_wo, L1_gnn_bo):
    import numpy as np
    import concourse.bacc as bacc
    from concourse.bass_utils import run_bass_kernel_spmd

    def rows(a):
        return np.tile(np.asarray(a)[None, :], (P, 1))

    def columns(a):
        return np.asarray(a).reshape(-1, P).T

    def turned(a):
        return np.asarray(a).T

    given = [
        ("x", x), ("adj", adj), ("w1", L0_gnn_mlp1_w), ("b1", columns(L0_gnn_mlp1_b)), ("w2", L0_gnn_mlp2_w),
        ("b2", L0_gnn_mlp2_b), ("wfc", L0_gnn_W_fc), ("wfcT", turned(L0_gnn_W_fc)),
        ("afc", np.asarray(L0_gnn_a_fc).reshape(2, -1, P).transpose(2, 1, 0)), ("wh", L0_gnn_W_hand), ("whT", turned(L0_gnn_W_hand)),
        ("ah", columns(L0_gnn_a_hand)), ("wqT", turned(L1_gnn_wq)), ("bq", L1_gnn_bq),
        ("wkT", turned(L1_gnn_wk)), ("bk", L1_gnn_bk), ("wvT", turned(L1_gnn_wv)), ("bv", rows(L1_gnn_bv)),
        ("woT", turned(L1_gnn_wo)), ("bo", rows(L1_gnn_bo)), ("eye", np.eye(P, dtype=np.float32)),
    ]
    nc = bacc.Bacc("TRN2", target_bir_lowering=False, num_devices=1)
    arrays, args = {}, []
    for name, a in given:
        a = np.ascontiguousarray(a)
        arrays[f"in_{name}"] = a
        args.append(nc.dram_tensor(f"in_{name}", a.shape, mybir.dt.from_np(a.dtype), kind="ExternalInput").ap())
    shape = arrays["in_x"].shape
    args.append(nc.dram_tensor("out_y", shape, F32, kind="ExternalOutput").ap())
    build(nc, *args)
    r = run_bass_kernel_spmd(nc, [arrays], core_ids=[0])
    return r.results[0]["out_y"]
```

```python
from contextlib import ExitStack

import concourse.bass as bass
from concourse import mybir

ALU = mybir.AluOpType
ACT = mybir.ActivationFunctionType
AX = mybir.AxisListType
F32 = mybir.dt.float32
F16 = mybir.dt.float16
BF16 = mybir.dt.bfloat16
I32 = mybir.dt.int32

P = 128
BANK = 512
ALPHA = 0.2
R_TOP = 75.0
MASKED = -1.0e30
GAT_ONLY = -(2.0 ** -100)
M_TOP = 60000.0
TINY = 1.0e-30
EPS = 1.0e-5


class Signal:

    def __init__(self, ctx, nc, name, per, first=0):
        self.sem, self.per, self.first = ctx.enter_context(nc.semaphore(name)), per, first

    def at(self, b, n):
        return b * self.per + (n + self.first)


class Fills:

    def __init__(self, order):
        self.first, self.reader, self.nth = {}, [], []
        for name, count, reader in order:
            self.first[name] = len(self.reader)
            for _ in range(count):
                self.nth.append(self.reader.count(reader))
                self.reader.append(reader)
        self.total = len(self.reader)

    def index(self, name, k=0):
        return self.first[name] + k

    def emptied(self, n):
        return self.nth[n] + 1

    def count(self, reader):
        return self.reader.count(reader)


def build(nc, x, adj, w1, b1, w2, b2, wfc, wfcT, afc, wh, whT, ah, wqT, bq, wkT, bk, wvT, bv, woT, bo, eye, out):
    B, N, D = x.shape
    NT = N // P
    NC = N // BANK
    TC = BANK // P
    F = w1.shape[1]
    FK = F // P
    H = 4
    HD = D // H
    GW = F + 1
    HW = D + 1
    SCALE = float(HD) ** -0.5
    KS = 3 * HD
    assert D == P and FK == 2 and NC == 2

    XF = Fills([("xT", NC, "act"), ("r1", FK * NC, "act"), ("h", NT, "act"), ("top1", 1, "dve"),
                ("f1", NC, "dve"), ("att1", NT, "dve"), ("zT", FK * NC, "dve"), ("r2", NC, "act"),
                ("h2", NT // 2, "act"), ("top2", 1, "dve"), ("f12", NC, "dve"), ("hm", 1, "dve"),
                ("att2", NT // 2, "dve"), ("r2n", NC, "dve")])
    SF = Fills([("x1T", 1, "act"), ("q", 1, "dve"), ("k", 1, "dve"), ("v", 1, "dve"), ("max", H * NT, "dve"),
                ("st", NC * NT * 2, "act"), ("on", 1, "dve"), ("onT", 1, "act"), ("proj", 1, "dve")])

    Z_AT, R2_AT, H2_AT, F2_AT, ATT2_AT = 1, 3, 4, 5, 8
    AHEAD = 2

    def att1_through(n):
        return AHEAD * NT + (n + 1) * (NT - AHEAD) * NT // (H * NT)

    with ExitStack() as ctx:
        def sb(name, shape, dt=F32):
            return ctx.enter_context(nc.sbuf_tensor(name, shape, dt))

        def ps(name, shape, dt=F32):
            return ctx.enter_context(nc.psum_tensor(name, shape, dt))

        def signal(name, per=1, first=0):
            return Signal(ctx, nc, name, per, first)

        ident = sb("ident", [P, P])
        identb = sb("identb", [P, P], BF16)
        ones = sb("ones", [P, P])
        headsel = sb("headsel", [P, H])
        w1s = sb("w1s", [P, F])
        w2s = sb("w2s", [P, FK, D])
        wfx = sb("wfx", [P, FK, GW])
        wfTs = sb("wfTs", [P, FK, F])
        wa1 = sb("wa1", [P, FK, P])
        whx = sb("whx", [P, HW])
        whTs = sb("whTs", [P, D])
        wh1 = sb("wh1", [P, P])
        afs = sb("afs", [P, FK, 2])
        ahs = sb("ahs", [P, 2])
        b1s = sb("b1s", [P, FK])
        b2s = sb("b2s", [P, 1])
        wqs, wks, wvs, wos = (sb(n, [P, D]) for n in ("wqs", "wks", "wvs", "wos"))
        bqs, bks = sb("bqs", [P, 1]), sb("bks", [P, 1])
        bvs, bos = sb("bvs", [P, D]), sb("bos", [P, D])
        mask = sb("mask", [P, NT, N], BF16)
        maskT = sb("maskT", [P, NT, N], BF16)
        neg = sb("neg", [P, N], BF16)
        rowtop = sb("rowtop", [P, NT])
        dead = sb("dead", [P, NT])
        half = sb("half", [P, NT])
        minus1 = sb("minus1", [P, 1])
        xin = sb("xin", [P, NT, D])
        xT = sb("xT", [P, N])
        r1T = sb("r1T", [P, FK, N])
        hx = sb("hx", [P, NT, GW + 1])
        r2T = sb("r2T", [P, N])
        r2sum = sb("r2sum", [P, NC])
        h2x = sb("h2x", [P, NT, HW + 1])
        r2bc = sb("r2bc", [P, P])
        hmean = sb("hmean", [P, D])
        f2top = sb("f2top", [P, 1])
        diag = sb("diag", [P, P])
        top = sb("top", [P, 3])
        uv = sb("uv", [P, 2, NT])
        rrep = sb("rrep", [P, N])
        pw = sb("pw", [P, NT, N])

        rden = sb("rden", [P, NT])
        att = sb("att", [P, NT, F])
        el = sb("el", [P, NT, F])
        stat = sb("stat", [P, 8, NT])
        x1 = sb("x1", [P, NT, D])
        x1T = sb("x1T", [P, N])
        qkhi = sb("qkhi", [P, 2, N], F16)
        qklo = sb("qklo", [P, 2, N], F16)
        qst = sb("qst", [KS + 1, H, N], F16)
        kst = sb("kst", [KS + 1, H, N], F16)
        vs = sb("vs", [P, NT, D])
        junk = sb("junk", [P, N], BF16)
        mx = sb("mx", [P, H * NT])
        mrow = sb("mrow", [H * NT, P], F16)
        pt = sb("pt", [P, 2, H, BANK])
        oT = sb("oT", [P, N])
        dT = sb("dT", [P, N])
        sq2 = dT[:, :].rearrange("p (t d) -> p t d", d=D)
        dn = sb("dn", [P, NT, H])
        on = sb("on", [P, NT, D])
        y2 = sb("y2", [P, NT, D])
        stat2 = sb("stat2", [P, 8, NT])
        px = [ps(f"px{n}", [P, BANK]) for n in range(2)]
        pss = [ps(f"pss{n}", [P, N]) for n in range(2)]
        po = ps("po", [P, BANK])
        pd = ps("pd", [P, BANK])

        s_w = signal("s_w")
        s_adj = signal("s_adj")
        s_const = signal("s_const")
        s_neg = signal("s_neg")
        s_mask = signal("s_mask")
        s_dead = signal("s_dead")
        s_mtr = signal("s_mtr")
        s_mtc = signal("s_mtc")
        s_wa = signal("s_wa")
        s_wac = signal("s_wac")
        s_xin = signal("s_xin", 16)
        x_full = signal("x_full", XF.total)
        x_act = signal("x_act", XF.count("act"), 1)
        x_dve = signal("x_dve", XF.count("dve"), 1)
        s_f2top = signal("s_f2top", 2)
        s_diag = signal("s_diag", 2)
        s_topn = signal("s_topn", 4)
        s_uv = signal("s_uv", 4)
        s_r = signal("s_r", 2 * NC)
        s_p1 = signal("s_p1", NT)
        s_p2 = signal("s_p2", 2 * NT)
        s_rden = signal("s_rden", NT)
        s_min = signal("s_min", 3)
        s_e1 = signal("s_e1", 3)
        s_e2 = signal("s_e2", 3)
        s_z = signal("s_z", 3)
        s_bc = signal("s_bc", 2)
        s_den2 = signal("s_den2", 2 * (NT // 2))
        s_x2 = signal("s_x2", NT)
        s_y = signal("s_y", NC, 1)
        s_ln = signal("s_ln", 10)
        s_sq = signal("s_sq", 1)
        s_pow = signal("s_pow", 1)
        s_full = signal("s_full", SF.total)
        f_act = signal("f_act", SF.count("act"), 1)
        f_dve = signal("f_dve", SF.count("dve"), 1)
        s_hi = signal("s_hi", 2)
        s_stq = signal("s_stq", 16 * 3 * H)
        s_stk = signal("s_stk", 16 * 3 * H)
        s_go = signal("s_go", H * NT)
        s_mxT = signal("s_mxT", 1)
        s_mrow = signal("s_mrow", 1)
        s_mdma = signal("s_mdma", 16)
        s_pv = signal("s_pv", NC * NT, 1)
        s_oT = signal("s_oT", 2 * NC)
        s_dn = signal("s_dn", 1)
        s_dnr = signal("s_dnr", 2)
        s_y2 = signal("s_y2", 1)
        s_ln2 = signal("s_ln2", 10)
        s_sq2 = signal("s_sq2", 1)
        s_pow2 = signal("s_pow2", 1)
        s_out = signal("s_out", 16, 1)

        x_nat = x.rearrange("b (t p) d -> b p t d", p=P)
        o_nat = out.rearrange("b (t p) d -> b p t d", p=P)
        N_W = 18
        CONSTS = 7

        block = ctx.enter_context(nc.Block())

        @block.sync
        def _(sp):
            sp.sem_inc(s_out.sem, 1)
            sp.dma_start(pw[:, :, :].bitcast(I32), adj.rearrange("(t p) j -> p t j", p=P)).then_inc(s_adj.sem, 16)
            for dst, src in (
                (ident[:, :], eye), (w1s[:, :], w1), (b1s[:, :], b1),
                (wfx[:, :, 1:GW], wfc.rearrange("(k p) f -> p k f", p=P)),
                (wfTs[:, :, :], wfcT.rearrange("(k p) f -> p k f", p=P)),
                (afs[:, :, :], afc),
                (w2s[:, :, :], w2.rearrange("(k p) f -> p k f", p=P)),
                (b2s[:, :], b2.rearrange("(p o) -> p o", o=1)),
                (whx[:, 1:HW], wh), (whTs[:, :], whT),
                (ahs[:, :], ah),
                (wqs[:, :], wqT), (wks[:, :], wkT), (wvs[:, :], wvT), (wos[:, :], woT),
                (bqs[:, :], bq.rearrange("(p o) -> p o", o=1)), (bks[:, :], bk.rearrange("(p o) -> p o", o=1)),
                (bvs[:, :], bv), (bos[:, :], bo),
            ):
                sp.dma_start(dst, src).then_inc(s_w.sem, 16)

            def load_x(b):
                sp.wait_ge(s_y.sem, s_y.at(b, 0))
                sp.dma_start(xin[:, :, :], x_nat[b]).then_inc(s_xin.sem, 16)

            def stack(b):
                for n, (st, parts, sig) in enumerate(((qst, (qkhi, qklo, qkhi), s_stq),
                                                      (kst, (qkhi, qkhi, qklo), s_stk))):
                    sp.wait_ge(f_dve.sem, f_dve.at(b, SF.emptied(SF.index("q", n))))
                    for g, part in enumerate(parts):
                        for h in range(H):
                            sp.dma_start(st[g * HD:(g + 1) * HD, h, :],
                                         part[h * HD:(h + 1) * HD, n, :]).then_inc(sig.sem, 16)
                sp.wait_ge(s_mrow.sem, s_mrow.at(b, 1))
                sp.dma_start(qst[KS:KS + 1, :, :].rearrange("o h (t c) -> o (h t) c", c=P),
                             mrow[:, :]).then_inc(s_mdma.sem, 16)

            def store(b):
                sp.wait_ge(s_ln2.sem, s_ln2.at(b, 10))
                sp.dma_start(o_nat[b], y2[:, :, :]).then_inc(s_out.sem, 16)

            load_x(0)
            load_x(1)
            with sp.Fori(0, B - 2) as b:
                stack(b)
                load_x(b + 2)
                store(b)
            for b in (B - 2, B - 1):
                stack(b)
                store(b)
            sp.wait_ge(s_out.sem, 16 * B + 1)

        @block.gpsimd
        def _(pool):
            for n, (dst, value) in enumerate(((ones[:, :], 1.0), (hx[:, :, GW:GW + 1], 1.0), (h2x[:, :, HW:HW + 1], 1.0),
                                              (kst[KS:KS + 1, :, :], -1.0), (half[:, :], -0.5))):
                nc.gpsimd.memset(dst, value).then_inc(s_const.sem, 1)
                pool.wait_ge(s_const.sem, n + 1)
            pool.wait_ge(s_w.sem, 16 * (N_W + 1))
            nc.gpsimd.tensor_copy(headsel[:, :], ident[:, 0:P:HD]).then_inc(s_const.sem, 1)
            pool.wait_ge(s_const.sem, CONSTS - 1)
            nc.gpsimd.tensor_copy(identb[:, :], ident[:, :]).then_inc(s_const.sem, 1)
            pool.wait_ge(s_const.sem, CONSTS)

            def power(b, st, ln, done):
                pool.wait_ge(ln.sem, ln.at(b, 5))
                nc.gpsimd.tensor_tensor(st[:, 3, :], st[:, 2, :], half[:, :], ALU.pow).then_inc(done.sem, 1)

            power(0, stat, s_ln, s_pow)
            with pool.Fori(0, B - 1) as b:
                power(b + 1, stat, s_ln, s_pow)
                power(b, stat2, s_ln2, s_pow2)
            power(B - 1, stat2, s_ln2, s_pow2)

        @block.scalar
        def _(act):
            act.sem_inc(x_act.sem, 1)
            act.sem_inc(f_act.sem, 1)
            for jt in range(NT):
                act.wait_ge(s_mtr.sem, jt + 1)
                nc.scalar.activation(maskT[:, jt, :], px[jt % 2][:, :].bitcast(BF16), ACT.Copy).then_inc(s_mtc.sem, 1)

            def x_filled(b, name, k=0):
                act.wait_ge(x_full.sem, x_full.at(b, XF.index(name, k) + 1))

            def elus(b, n, part):
                act.wait_ge(s_min.sem, s_min.at(b, n + 1))
                nc.scalar.activation(part, part, ACT.Exp).then_inc(s_e1.sem, 1)
                act.wait_ge(s_e1.sem, s_e1.at(b, n + 1))
                nc.scalar.activation(part, part, ACT.Exp, bias=minus1[:, :]).then_inc(s_e2.sem, 1)

            def powers(b, n, hxt):
                act.wait_ge(s_topn.sem, s_topn.at(b, 2 * n + 2))
                if n == 1:
                    act.wait_ge(s_p1.sem, s_p1.at(b, NT))
                nc.scalar.activation(uv[:, 0, :], hxt[:, :, 0], ACT.Exp, bias=top[:, 1:2]).then_inc(s_uv.sem, 1)
                nc.scalar.activation(uv[:, 1, :], hxt[:, :, 0], ACT.Exp, bias=top[:, 2:3],
                                     scale=ALPHA).then_inc(s_uv.sem, 1)

            def factors(b, n):
                for c in range(NC):
                    k = XF.emptied(XF.index(("f1", "f12")[n], c))
                    act.wait_ge(x_dve.sem, x_dve.at(b, k))
                    nc.scalar.activation(rrep[:, c * BANK:(c + 1) * BANK], rrep[:, c * BANK:(c + 1) * BANK],
                                         ACT.Exp, scale=1.0 - ALPHA).then_inc(s_r.sem, 1)

            act.wait_ge(s_w.sem, 16 * (N_W + 1))
            act.wait_ge(s_const.sem, CONSTS)
            act.wait_ge(s_wac.sem, 4)

            def square(b, ln, done, dst, src):
                act.wait_ge(ln.sem, ln.at(b, 3))
                nc.scalar.activation(dst, src, ACT.Square).then_inc(done.sem, 1)

            def exps(b, s):
                jt = s % NT
                act.wait_ge(s_pv.sem, s_pv.at(b, max(s - 1, 0)))
                for hp in range(2):
                    n = 2 * s + hp
                    act.wait_ge(s_full.sem, s_full.at(b, SF.index("st", n) + 1))
                    nc.scalar.activation(pt[:, jt % 2, 2 * hp:2 * hp + 2, :].rearrange("p h c -> p (h c)"),
                                         pss[SF.index("st", n) % 2][:, :], ACT.Exp, scale=SCALE).then_inc(f_act.sem, 1)

            def body(b1, b0):
                if b0 is not None:
                    for c in range(NC):
                        x_filled(b0, "xT", c)
                        nc.scalar.activation(xT[:, c * BANK:(c + 1) * BANK], px[XF.index("xT", c) % 2][:, :],
                                             ACT.Copy).then_inc(x_act.sem, 1)
                    for k in range(FK):
                        for c in range(NC):
                            n = k * NC + c
                            x_filled(b0, "r1", n)
                            nc.scalar.activation(r1T[:, k, c * BANK:(c + 1) * BANK],
                                                 px[XF.index("r1", n) % 2][:, :],
                                                 ACT.Relu, bias=b1s[:, k:k + 1]).then_inc(x_act.sem, 1)
                    for jt in range(NT):
                        x_filled(b0, "h", jt)
                        nc.scalar.activation(hx[:, jt, 0:GW], px[XF.index("h", jt) % 2][:, 0:GW],
                                             ACT.Copy).then_inc(x_act.sem, 1)
                if b1 is not None:
                    act.wait_ge(s_full.sem, s_full.at(b1, SF.index("x1T") + 1))
                    nc.scalar.activation(x1T[:, :], pss[SF.index("x1T") % 2][:, :], ACT.Copy).then_inc(f_act.sem, 1)
                if b0 is not None:
                    powers(b0, 0, hx)
                if b1 is not None:
                    act.wait_ge(s_full.sem, s_full.at(b1, SF.index("q") + 1))
                    nc.scalar.activation(qkhi[:, 0, :], pss[SF.index("q") % 2][:, :], ACT.Identity,
                                         bias=bqs[:, :]).then_inc(s_hi.sem, 1)
                if b0 is not None:
                    factors(b0, 0)
                if b1 is not None:
                    act.wait_ge(s_full.sem, s_full.at(b1, SF.index("k") + 1))
                    nc.scalar.activation(qkhi[:, 1, :], pss[SF.index("k") % 2][:, :], ACT.Identity,
                                         bias=bks[:, :]).then_inc(s_hi.sem, 1)
                if b0 is not None:
                    for n in range(2):
                        elus(b0, n, el[:, n * NT // 2:(n + 1) * NT // 2, :])
                for s in range(NC * NT):
                    if b1 is not None:
                        exps(b1, s)
                    if b0 is not None and s == R2_AT:
                        for c in range(NC):
                            x_filled(b0, "r2", c)
                            nc.scalar.activation(r2T[:, c * BANK:(c + 1) * BANK], px[XF.index("r2", c) % 2][:, :],
                                                 ACT.Relu, bias=b2s[:, :],
                                                 accum_out=r2sum[:, c:c + 1]).then_inc(x_act.sem, 1)
                    if b0 is not None and s == H2_AT:
                        for n in range(NT // 2):
                            x_filled(b0, "h2", n)
                            nc.scalar.activation(
                                h2x[:, 2 * n:2 * n + 2, 0:HW],
                                px[XF.index("h2", n) % 2][:, 0:2 * HW].rearrange("p (t f) -> p t f", t=2),
                                ACT.Copy).then_inc(x_act.sem, 1)
                    if b0 is not None and s == F2_AT + 1:
                        powers(b0, 1, h2x)
                        factors(b0, 1)
                if b1 is not None:
                    act.wait_ge(s_full.sem, s_full.at(b1, SF.index("onT") + 1))
                    nc.scalar.activation(oT[:, :], pss[SF.index("onT") % 2][:, :], ACT.Copy).then_inc(f_act.sem, 1)
                if b0 is not None:
                    elus(b0, 2, el[:, 0:NT // 2, :])
                    square(b0, s_ln, s_sq, el[:, 0:NT // 2, :].rearrange("p t f -> p (t f)"),
                           att[:, NT // 2:NT, :].rearrange("p t f -> p (t f)"))
                if b1 is not None:
                    square(b1, s_ln2, s_sq2, dT[:, :], on[:, :, :].rearrange("p t f -> p (t f)"))

            body(None, 0)
            with act.Fori(0, B - 1) as b:
                body(b, b + 1)
            body(B - 1, None)

        @block.vector
        def _(dve):
            dve.sem_inc(x_dve.sem, 1)
            dve.sem_inc(f_dve.sem, 1)
            dve.sem_inc(s_y.sem, 1)
            nc.vector.memset(minus1[:, :], -1.0).then_inc(s_dead.sem, 1)
            dve.wait_ge(s_adj.sem, 16)
            for it in range(NT):
                a = pw[:, it, :].bitcast(I32)
                if it:
                    dve.wait_ge(s_mask.sem, 2 * it)
                nc.vector.tensor_scalar(neg[:, :], a, 0, GAT_ONLY, ALU.is_lt, ALU.mult).then_inc(s_neg.sem, 1)
                nc.vector.tensor_scalar(mask[:, it, :], a, 0, MASKED, ALU.is_equal, ALU.mult).then_inc(s_mask.sem, 1)
                dve.wait_ge(s_neg.sem, it + 1)
                dve.wait_ge(s_mask.sem, 2 * it + 1)
                nc.vector.tensor_tensor(mask[:, it, :], mask[:, it, :], neg[:, :], ALU.add).then_inc(s_mask.sem, 1)
            for it in range(NT):
                dve.wait_ge(s_mask.sem, 2 * it + 2)
                nc.vector.reduce_max(rowtop[:, it:it + 1], mask[:, it, :], axis=AX.X).then_inc(s_dead.sem, 1)
            dve.wait_ge(s_dead.sem, NT + 1)
            nc.vector.tensor_scalar(dead[:, :], rowtop[:, :], 0.0, None, ALU.is_lt).then_inc(s_dead.sem, 1)
            dve.wait_ge(s_wa.sem, FK + 1)
            for k in range(FK):
                nc.vector.tensor_copy(wfx[:, k, 0:1], po[:, 2 * k + 1:2 * k + 2]).then_inc(s_wac.sem, 1)
                nc.vector.tensor_scalar(wa1[:, k, :], ones[:, :], po[:, 2 * k:2 * k + 1], None,
                                        ALU.mult).then_inc(s_dead.sem, 1)
            nc.vector.tensor_copy(whx[:, 0:1], po[:, 5:6]).then_inc(s_wac.sem, 1)
            nc.vector.tensor_scalar(wh1[:, :], ones[:, :], po[:, 4:5], None, ALU.mult).then_inc(s_wac.sem, 1)

            def x_filled(b, name, k=0):
                dve.wait_ge(x_full.sem, x_full.at(b, XF.index(name, k) + 1))
                return px[XF.index(name, k) % 2]

            def find_top(b, n, hxt):
                done = XF.emptied(XF.index(("h", "h2")[n], (NT, NT // 2)[n] - 1))
                dve.wait_ge(x_act.sem, x_act.at(b, done))
                nc.vector.reduce_max(f2top[:, :], hxt[:, :, 0], axis=AX.X).then_inc(s_f2top.sem, 1)
                dve.wait_ge(s_f2top.sem, s_f2top.at(b, n + 1))
                nc.vector.tensor_scalar(diag[:, :], ident[:, :], f2top[:, :], None, ALU.mult).then_inc(s_diag.sem, 1)
                src = x_filled(b, ("top1", "top2")[n])
                nc.vector.reduce_max(top[:, 0:1], src[:, 0:P], axis=AX.X).then_inc(x_dve.sem, 1)
                dve.wait_ge(x_dve.sem, x_dve.at(b, XF.emptied(XF.index(("top1", "top2")[n]))))
                nc.vector.tensor_scalar(top[:, 1:2], top[:, 0:1], -1.0, None, ALU.mult).then_inc(s_topn.sem, 1)
                nc.vector.tensor_scalar(top[:, 2:3], top[:, 0:1], -ALPHA, None, ALU.mult).then_inc(s_topn.sem, 1)
                for c in range(NC):
                    src = x_filled(b, ("f1", "f12")[n], c)
                    nc.vector.tensor_scalar(rrep[:, c * BANK:(c + 1) * BANK], src[:, :], top[:, 0:1], R_TOP,
                                            ALU.add, ALU.min).then_inc(x_dve.sem, 1)

            def norm_first(b, ln, sq_done, y, yc, sq, st):
                nc.vector.reduce_sum(st[:, 0, :], y, axis=AX.X).then_inc(ln.sem, 1)
                dve.wait_ge(ln.sem, ln.at(b, 1))
                nc.vector.tensor_scalar(st[:, 1, :], st[:, 0, :], 1.0 / D, None, ALU.mult).then_inc(ln.sem, 1)
                dve.wait_ge(ln.sem, ln.at(b, 2))
                nc.vector.tensor_tensor(yc, y, st[:, 1, :].unsqueeze(2).to_broadcast([P, NT, D]),
                                        ALU.subtract).then_inc(ln.sem, 1)
                dve.wait_ge(sq_done.sem, sq_done.at(b, 1))
                nc.vector.reduce_sum(st[:, 0, :], sq, axis=AX.X).then_inc(ln.sem, 1)
                dve.wait_ge(ln.sem, ln.at(b, 4))
                nc.vector.tensor_scalar(st[:, 2, :], st[:, 0, :], 1.0 / D, EPS, ALU.mult, ALU.add).then_inc(ln.sem, 1)

            def norm_second(b, ln, pow_done, yc, st, res):
                dve.wait_ge(pow_done.sem, pow_done.at(b, 1))
                nc.vector.tensor_tensor(st[:, 4, :], st[:, 3, :], st[:, 3, :], ALU.mult).then_inc(ln.sem, 1)
                dve.wait_ge(ln.sem, ln.at(b, 6))
                nc.vector.tensor_tensor(st[:, 5, :], st[:, 4, :], st[:, 2, :], ALU.mult).then_inc(ln.sem, 1)
                dve.wait_ge(ln.sem, ln.at(b, 7))
                nc.vector.tensor_scalar(st[:, 6, :], st[:, 5, :], -0.5, 1.5, ALU.mult, ALU.add).then_inc(ln.sem, 1)
                dve.wait_ge(ln.sem, ln.at(b, 8))
                nc.vector.tensor_tensor(st[:, 7, :], st[:, 3, :], st[:, 6, :], ALU.mult).then_inc(ln.sem, 1)
                dve.wait_ge(ln.sem, ln.at(b, 9))
                nc.vector.tensor_tensor(res, yc, st[:, 7, :].unsqueeze(2).to_broadcast([P, NT, D]),
                                        ALU.mult).then_inc(ln.sem, 1)

            def gat0_weights(b):
                dve.wait_ge(s_uv.sem, s_uv.at(b, 2))
                dve.wait_ge(s_r.sem, s_r.at(b, NC))
                for jt in range(NT):
                    nc.vector.tensor_scalar(pw[:, jt, :], rrep[:, :], uv[:, 0, jt:jt + 1], uv[:, 1, jt:jt + 1],
                                            ALU.mult, ALU.max).then_inc(s_p1.sem, 1)

            def halves(g):
                return slice(g * NT // 2, (g + 1) * NT // 2)

            def gat0_row(b, it):
                src = x_filled(b, "att1", it)
                nc.vector.reciprocal(rden[:, it:it + 1], src[:, F:F + 1]).then_inc(s_rden.sem, 1)
                dve.wait_ge(s_rden.sem, s_rden.at(b, it + 1))
                nc.vector.tensor_scalar(att[:, it, :], src[:, 0:F], rden[:, it:it + 1], None,
                                        ALU.mult).then_inc(x_dve.sem, 1)
                if it % (NT // 2) == NT // 2 - 1:
                    part = halves(it // (NT // 2))
                    dve.wait_ge(x_dve.sem, x_dve.at(b, XF.emptied(XF.index("att1", it))))
                    nc.vector.tensor_scalar(el[:, part, :], att[:, part, :], 0.0, None, ALU.min).then_inc(s_min.sem, 1)

            def gat0_elu(b, g):
                part = halves(g)
                dve.wait_ge(s_e2.sem, s_e2.at(b, g + 1))
                nc.vector.scalar_tensor_tensor(
                    att[:, part, :].rearrange("p t f -> p (t f)"),
                    att[:, part, :].rearrange("p t f -> p (t f)"), 0.0,
                    el[:, part, :].rearrange("p t f -> p (t f)"), ALU.max, ALU.add).then_inc(s_z.sem, 1)

            def residual0(b):
                for n in range(FK * NC):
                    k, c = n % FK, n // FK
                    src = x_filled(b, "zT", n)
                    r = r1T[:, k, c * BANK:(c + 1) * BANK]
                    nc.vector.scalar_tensor_tensor(r, src[:, :], -1.0, r, ALU.add, ALU.add).then_inc(x_dve.sem, 1)

            def gat1_weights(b):
                find_top(b, 1, h2x)
                nc.vector.tensor_tensor(r2sum[:, 0:1], r2sum[:, 0:1], r2sum[:, 1:2], ALU.add).then_inc(s_bc.sem, 1)
                dve.wait_ge(s_bc.sem, s_bc.at(b, 1))
                nc.vector.tensor_scalar(r2bc[:, :], ones[:, :], r2sum[:, 0:1], 1.0 / N, ALU.mult,
                                        ALU.mult).then_inc(s_bc.sem, 1)
                src = x_filled(b, "hm")
                nc.vector.tensor_copy(hmean[:, :], src[:, 0:D]).then_inc(x_dve.sem, 1)
                dve.wait_ge(s_uv.sem, s_uv.at(b, 4))
                dve.wait_ge(s_r.sem, s_r.at(b, 2 * NC))
                for jt in range(NT):
                    nc.vector.tensor_scalar(pw[:, jt, :], rrep[:, :], uv[:, 0, jt:jt + 1], uv[:, 1, jt:jt + 1],
                                            ALU.mult, ALU.max).then_inc(s_p2.sem, 1)
                    dve.wait_ge(s_p2.sem, s_p2.at(b, 2 * jt + 1))
                    nc.vector.scalar_tensor_tensor(pw[:, jt, :], maskT[:, jt, :], 0.0, pw[:, jt, :],
                                                   ALU.is_ge, ALU.mult).then_inc(s_p2.sem, 1)

            x2 = att[:, 0:NT // 2, :].rearrange("p t f -> p (t f)").rearrange("p (t f) -> p t f", t=NT)
            e2 = el[:, 0:NT // 2, :].rearrange("p t f -> p (t f)").rearrange("p (t f) -> p t f", t=NT)
            yc = att[:, NT // 2:NT, :].rearrange("p t f -> p (t f)").rearrange("p (t f) -> p t f", t=NT)

            def gat1_rows(b, n):
                tt = slice(2 * n, 2 * n + 2)
                src = x_filled(b, "att2", n)[:, 0:2 * HW].rearrange("p (t f) -> p t f", t=2)
                nc.vector.tensor_scalar(rden[:, tt], src[:, :, D], TINY, None, ALU.max).then_inc(s_den2.sem, 1)
                dve.wait_ge(s_den2.sem, s_den2.at(b, 2 * n + 1))
                nc.vector.reciprocal(rden[:, tt], rden[:, tt]).then_inc(s_den2.sem, 1)
                dve.wait_ge(s_den2.sem, s_den2.at(b, 2 * n + 2))
                nc.vector.tensor_tensor(x2[:, tt, :], src[:, :, 0:D], rden[:, tt].unsqueeze(2).to_broadcast([P, 2, D]),
                                        ALU.mult).then_inc(x_dve.sem, 1)
                dve.wait_ge(x_dve.sem, x_dve.at(b, XF.emptied(XF.index("att2", n))))
                for it in range(2 * n, 2 * n + 2):
                    nc.vector.scalar_tensor_tensor(x2[:, it, :], hmean[:, :], dead[:, it:it + 1], x2[:, it, :],
                                                   ALU.mult, ALU.add).then_inc(s_x2.sem, 1)

            def gat1_min(b):
                dve.wait_ge(s_x2.sem, s_x2.at(b, NT))
                nc.vector.tensor_scalar(e2, x2, 0.0, None, ALU.min).then_inc(s_min.sem, 1)

            def residual1(b):
                dve.wait_ge(s_e2.sem, s_e2.at(b, 3))
                nc.vector.scalar_tensor_tensor(x2, x2, 0.0, e2, ALU.max, ALU.add).then_inc(s_z.sem, 1)
                dve.wait_ge(s_z.sem, s_z.at(b, 3))
                for c in range(NC):
                    src = x_filled(b, "r2n", c)[:, :].rearrange("p (t f) -> p t f", f=D)
                    tt = slice(c * TC, (c + 1) * TC)
                    nc.vector.scalar_tensor_tensor(x2[:, tt, :], src, -1.0, x2[:, tt, :], ALU.add,
                                                   ALU.add).then_inc(x_dve.sem, 1)
                    dve.wait_ge(x_dve.sem, x_dve.at(b, XF.emptied(XF.index("r2n", c))))
                    nc.vector.scalar_tensor_tensor(x2[:, tt, :], x2[:, tt, :], 0.0, xin[:, tt, :], ALU.max,
                                                   ALU.add).then_inc(s_y.sem, 1)
                dve.wait_ge(s_y.sem, s_y.at(b, NC))

            def low_half(b, n, bias):
                dve.wait_ge(s_hi.sem, s_hi.at(b, n + 1))
                nc.vector.scalar_tensor_tensor(qklo[:, n, :], pss[SF.index("q", n) % 2][:, :], bias[:, :],
                                               qkhi[:, n, :], ALU.add, ALU.subtract).then_inc(f_dve.sem, 1)

            def values(b):
                dve.wait_ge(s_full.sem, s_full.at(b, SF.index("v") + 1))
                nc.vector.tensor_tensor(vs[:, :, :], pss[SF.index("v") % 2][:, :].rearrange("p (t f) -> p t f", f=D),
                                        bvs[:, :].unsqueeze(1).to_broadcast([P, NT, D]),
                                        ALU.add).then_inc(f_dve.sem, 1)

            def row_max(b, n):
                m = SF.index("max", n)
                dve.wait_ge(f_dve.sem, f_dve.at(b, SF.emptied(m) - 1))
                dve.wait_ge(s_full.sem, s_full.at(b, m + 1))
                dve.sem_inc(s_go.sem, 1)
                nc.vector.tensor_tensor_reduce(out=junk[:, :], in0=pss[m % 2][:, :], in1=mask[:, n % NT, :],
                                               scale=1.0, scalar=-3.0e38, op0=ALU.add, op1=ALU.max,
                                               accum_out=mx[:, n:n + 1]).then_inc(f_dve.sem, 1)

            def max_row(b):
                dve.wait_ge(s_mxT.sem, s_mxT.at(b, 1))
                nc.vector.tensor_scalar(mrow[:, :], po[0:H * NT, 0:P], -M_TOP, M_TOP, ALU.max,
                                        ALU.min).then_inc(s_mrow.sem, 1)

            def accumulated(b, c):
                cc = slice(c * BANK, (c + 1) * BANK)
                dve.wait_ge(s_pv.sem, s_pv.at(b, (c + 1) * NT))
                nc.vector.tensor_copy(oT[:, cc], po[:, :]).then_inc(s_oT.sem, 1)
                nc.vector.tensor_copy(dT[:, cc], pd[:, :]).then_inc(s_oT.sem, 1)

            def divided(b):
                dve.wait_ge(s_dn.sem, s_dn.at(b, 1))
                nc.vector.tensor_scalar(dn[:, :, :], pd[:, 0:NT * H].rearrange("p (t h) -> p t h", h=H), TINY, None,
                                        ALU.max).then_inc(s_dnr.sem, 1)
                dve.wait_ge(s_dnr.sem, s_dnr.at(b, 1))
                nc.vector.reciprocal(dn[:, :, :], dn[:, :, :]).then_inc(s_dnr.sem, 1)
                dve.wait_ge(s_dnr.sem, s_dnr.at(b, 2))
                dve.wait_ge(s_full.sem, s_full.at(b, SF.index("on") + 1))
                nc.vector.tensor_tensor(on[:, :, :].rearrange("p t (h d) -> p (t h) d", h=H),
                                        pss[SF.index("on") % 2][:, :].rearrange("p (g d) -> p g d", d=HD),
                                        dn[:, :, :].rearrange("p t h -> p (t h)").unsqueeze(2)
                                        .to_broadcast([P, NT * H, HD]), ALU.mult).then_inc(f_dve.sem, 1)

            def residual2(b):
                dve.wait_ge(s_full.sem, s_full.at(b, SF.index("proj") + 1))
                dve.wait_ge(s_out.sem, s_out.at(b, 0))
                nc.vector.tensor_tensor(y2[:, :, :], pss[SF.index("proj") % 2][:, :].rearrange("p (t f) -> p t f", f=D),
                                        x1[:, :, :], ALU.add).then_inc(f_dve.sem, 1)
                dve.wait_ge(f_dve.sem, f_dve.at(b, SF.count("dve")))
                nc.vector.tensor_tensor(y2[:, :, :], y2[:, :, :], bos[:, :].unsqueeze(1).to_broadcast([P, NT, D]),
                                        ALU.add).then_inc(s_y2.sem, 1)
                dve.wait_ge(s_y2.sem, s_y2.at(b, 1))

            def body(b1, b0):
                if b0 is not None:
                    find_top(b0, 0, hx)
                if b1 is not None:
                    low_half(b1, 0, bqs)
                if b0 is not None:
                    gat0_weights(b0)
                if b1 is not None:
                    low_half(b1, 1, bks)
                    values(b1)
                if b0 is not None:
                    for it in range(AHEAD):
                        gat0_row(b0, it)
                for n in range(H * NT):
                    if b1 is not None:
                        row_max(b1, n)
                    if b0 is not None:
                        for it in range(att1_through(n - 1) // NT, att1_through(n) // NT):
                            gat0_row(b0, it)
                        if n == H * NT * 3 // 4:
                            gat0_elu(b0, 0)
                if b1 is not None:
                    max_row(b1)
                if b0 is not None:
                    gat0_elu(b0, 1)
                    residual0(b0)
                    gat1_weights(b0)
                for c in range(NC):
                    if b1 is not None:
                        accumulated(b1, c)
                    if b0 is not None and c < NC - 1:
                        for n in range(NT // 2):
                            gat1_rows(b0, n)
                        gat1_min(b0)
                if b1 is not None:
                    divided(b1)
                if b0 is not None:
                    residual1(b0)
                    norm_first(b0, s_ln, s_sq, x2, yc, e2, stat)
                if b1 is not None:
                    residual2(b1)
                if b0 is not None:
                    norm_second(b0, s_ln, s_pow, yc, stat, x1[:, :, :])
                if b1 is not None:
                    norm_first(b1, s_ln2, s_sq2, y2[:, :, :], on[:, :, :], sq2, stat2)
                    norm_second(b1, s_ln2, s_pow2, on[:, :, :], stat2, y2[:, :, :])

            dve.wait_ge(s_w.sem, 16 * (N_W + 1))
            dve.wait_ge(s_const.sem, CONSTS)
            dve.wait_ge(s_dead.sem, NT + 2 + FK)
            body(None, 0)
            with dve.Fori(0, B - 1) as b:
                body(b, b + 1)
            body(B - 1, None)

        @block.tensor
        def _(pe):
            pe.sem_inc(s_pv.sem, 1)
            pe.wait_ge(s_w.sem, 16 * (N_W + 1))
            pe.wait_ge(s_const.sem, CONSTS)
            for k in range(FK):
                for f in range(FK):
                    last = nc.tensor.matmul(po[:, 2 * k:2 * k + 2], wfTs[:, f, k * P:(k + 1) * P], afs[:, f, :],
                                            start=(f == 0), stop=(f == FK - 1))
                last.then_inc(s_wa.sem, 1)
            nc.tensor.matmul(po[:, 4:6], whTs[:, :], ahs[:, :], start=True, stop=True).then_inc(s_wa.sem, 1)
            pe.wait_ge(s_mask.sem, 2 * NT)
            for jt in range(NT):
                if jt >= 2:
                    pe.wait_ge(s_mtc.sem, jt - 1)
                for it in range(NT):
                    last = nc.tensor.transpose(px[jt % 2][:, :].bitcast(BF16)[:, it * P:(it + 1) * P],
                                               mask[:, it, jt * P:(jt + 1) * P], identb[:, :])
                last.then_inc(s_mtr.sem, 1)
            pe.wait_ge(s_mtc.sem, NT)
            pe.wait_ge(s_wac.sem, 4)
            pe.wait_ge(s_dead.sem, NT + 2 + FK)

            def x_room(b, name, k=0):
                n = XF.index(name, k)
                if n < 2:
                    pe.wait_ge(x_act.sem, x_act.at(b, 0))
                elif XF.reader[n - 2] == "act":
                    pe.wait_ge(x_act.sem, x_act.at(b, XF.emptied(n - 2)))
                else:
                    pe.wait_ge(x_dve.sem, x_dve.at(b, XF.emptied(n - 2)))
                return px[n % 2]

            def s_room(b, name, k=0):
                n = SF.index(name, k)
                if n < 2:
                    pe.wait_ge(f_dve.sem, f_dve.at(b, 0))
                    pe.wait_ge(f_act.sem, f_act.at(b, 0))
                elif SF.reader[n - 2] == "act":
                    pe.wait_ge(f_act.sem, f_act.at(b, SF.emptied(n - 2)))
                else:
                    pe.wait_ge(f_dve.sem, f_dve.at(b, SF.emptied(n - 2)))
                return pss[n % 2]

            def emptied_act(b, name, k=0):
                pe.wait_ge(x_act.sem, x_act.at(b, XF.emptied(XF.index(name, k))))

            def node_top(b, n):
                dst = x_room(b, ("top1", "top2")[n])
                pe.wait_ge(s_diag.sem, s_diag.at(b, n + 1))
                nc.tensor.matmul(dst[:, 0:P], ones[:, :], diag[:, :], start=True, stop=True).then_inc(x_full.sem, 1)

            def f1_rows(b, n, w, src):
                for c in range(NC):
                    dst = x_room(b, ("f1", "f12")[n], c)
                    for k in range(len(w)):
                        last = nc.tensor.matmul(dst[:, :], w[k], src[k][:, c * BANK:(c + 1) * BANK],
                                                start=(k == 0), stop=(k == len(w) - 1))
                    last.then_inc(x_full.sem, 1)

            def first_mlp(b):
                pe.wait_ge(s_xin.sem, s_xin.at(b, 16))
                for c in range(NC):
                    dst = x_room(b, "xT", c)
                    for t in range(TC):
                        last = nc.tensor.transpose(dst[:, t * P:(t + 1) * P], xin[:, c * TC + t, :], ident[:, :])
                    last.then_inc(x_full.sem, 1)
                for k in range(FK):
                    for c in range(NC):
                        dst = x_room(b, "r1", k * NC + c)
                        emptied_act(b, "xT", c)
                        nc.tensor.matmul(dst[:, :], w1s[:, k * P:(k + 1) * P], xT[:, c * BANK:(c + 1) * BANK],
                                         start=True, stop=True).then_inc(x_full.sem, 1)
                emptied_act(b, "r1", FK * NC - 1)
                for jt in range(NT):
                    dst = x_room(b, "h", jt)
                    for k in range(FK):
                        last = nc.tensor.matmul(dst[:, 0:GW], r1T[:, k, jt * P:(jt + 1) * P], wfx[:, k, :],
                                                start=(k == 0), stop=(k == FK - 1))
                    last.then_inc(x_full.sem, 1)

            def att1(b, first, end):
                for m in range(first, end):
                    it, jt = m // NT, m % NT
                    if jt == 0:
                        x_room(b, "att1", it)
                    if it == 0:
                        pe.wait_ge(s_p1.sem, s_p1.at(b, jt + 1))
                    last = nc.tensor.matmul(px[XF.index("att1", it) % 2][:, 0:GW], pw[:, jt, it * P:(it + 1) * P],
                                            hx[:, jt, 1:GW + 1], start=(jt == 0), stop=(jt == NT - 1))
                    if jt == NT - 1:
                        last.then_inc(x_full.sem, 1)

            def turn_z(b, first, end):
                for n in range(first, end):
                    k, c = n % FK, n // FK
                    dst = x_room(b, "zT", n)
                    pe.wait_ge(s_z.sem, s_z.at(b, c + 1))
                    for t in range(TC):
                        last = nc.tensor.transpose(dst[:, t * P:(t + 1) * P],
                                                   att[:, c * TC + t, k * P:(k + 1) * P], ident[:, :])
                    last.then_inc(x_full.sem, 1)

            def second_mlp(b):
                for c in range(NC):
                    dst = x_room(b, "r2", c)
                    pe.wait_ge(x_dve.sem, x_dve.at(b, XF.emptied(XF.index("zT", FK * (c + 1) - 1))))
                    for k in range(FK):
                        last = nc.tensor.matmul(dst[:, :], w2s[:, k, :], r1T[:, k, c * BANK:(c + 1) * BANK],
                                                start=(k == 0), stop=(k == FK - 1))
                    last.then_inc(x_full.sem, 1)

            def second_h(b):
                for n in range(NT // 2):
                    dst = x_room(b, "h2", n)
                    emptied_act(b, "r2", 2 * n // TC)
                    for t in range(2):
                        jt = 2 * n + t
                        last = nc.tensor.matmul(dst[:, t * HW:(t + 1) * HW], r2T[:, jt * P:(jt + 1) * P], whx[:, :],
                                                start=True, stop=True)
                    last.then_inc(x_full.sem, 1)

            def mean_h(b):
                dst = x_room(b, "hm")
                pe.wait_ge(s_bc.sem, s_bc.at(b, 2))
                nc.tensor.matmul(dst[:, 0:D], r2bc[:, :], whx[:, 1:HW], start=True, stop=True).then_inc(x_full.sem, 1)

            def att2(b, it):
                if it % 2 == 0:
                    x_room(b, "att2", it // 2)
                dst = px[XF.index("att2", it // 2) % 2]
                t = it % 2
                for jt in range(NT):
                    if it == 0:
                        pe.wait_ge(s_p2.sem, s_p2.at(b, 2 * jt + 2))
                    last = nc.tensor.matmul(dst[:, t * HW:(t + 1) * HW], pw[:, jt, it * P:(it + 1) * P],
                                            h2x[:, jt, 1:HW + 1], start=(jt == 0), stop=(jt == NT - 1))
                if t == 1:
                    last.then_inc(x_full.sem, 1)

            def turn_r2(b):
                for c in range(NC):
                    dst = x_room(b, "r2n", c)
                    for t in range(TC):
                        n = c * TC + t
                        last = nc.tensor.transpose(dst[:, t * P:(t + 1) * P], r2T[:, n * P:(n + 1) * P], ident[:, :])
                    last.then_inc(x_full.sem, 1)

            def turn_x1(b):
                dst = s_room(b, "x1T")
                pe.wait_ge(s_ln.sem, s_ln.at(b, 10))
                for t in range(NT):
                    last = nc.tensor.transpose(dst[:, t * P:(t + 1) * P], x1[:, t, :], ident[:, :])
                last.then_inc(s_full.sem, 1)

            def queries_or_keys(b, n, w):
                dst = s_room(b, "q", n)
                pe.wait_ge(f_act.sem, f_act.at(b, SF.emptied(SF.index("x1T"))))
                for c in range(NC):
                    last = nc.tensor.matmul(dst[:, c * BANK:(c + 1) * BANK], w[:, :],
                                            x1T[:, c * BANK:(c + 1) * BANK], start=True, stop=True)
                last.then_inc(s_full.sem, 1)

            def values(b):
                dst = s_room(b, "v")
                for jt in range(NT):
                    last = nc.tensor.matmul(dst[:, jt * P:(jt + 1) * P], x1T[:, jt * P:(jt + 1) * P], wvs[:, :],
                                            start=True, stop=True)
                last.then_inc(s_full.sem, 1)

            def row_scores(b, n):
                h, it = n // NT, n % NT
                dst = s_room(b, "max", n)
                for c in range(NC):
                    last = nc.tensor.matmul(dst[:, c * BANK:(c + 1) * BANK], qst[0:KS, h, it * P:(it + 1) * P],
                                            kst[0:KS, h, c * BANK:(c + 1) * BANK], start=True, stop=True)
                last.then_inc(s_full.sem, 1)

            def turn_max(b):
                pe.wait_ge(f_dve.sem, f_dve.at(b, SF.emptied(SF.index("max", H * NT - 1))))
                nc.tensor.transpose(po[0:H * NT, 0:P], mx[:, :], ident[:, :]).then_inc(s_mxT.sem, 1)

            def scores(b, s):
                c, jt = s // NT, s % NT
                for hp in range(2):
                    dst = s_room(b, "st", 2 * s + hp)
                    for g in range(2):
                        h = 2 * hp + g
                        nc.tensor.matmul(dst[:, g * BANK:(g + 1) * BANK], kst[:, h, jt * P:(jt + 1) * P],
                                         qst[:, h, c * BANK:(c + 1) * BANK], start=True, stop=False)
                        last = nc.tensor.matmul(dst[:, g * BANK:(g + 1) * BANK], identb[:, :],
                                                maskT[:, jt, c * BANK:(c + 1) * BANK], start=False, stop=True)
                    last.then_inc(s_full.sem, 1)

            def products(b, s):
                c, jt = s // NT, s % NT
                pe.wait_ge(f_act.sem, f_act.at(b, SF.emptied(SF.index("st", 2 * s + 1))))
                if c > 0 and jt == 0:
                    pe.wait_ge(s_oT.sem, s_oT.at(b, 2 * c))
                for h in range(H):
                    nc.tensor.matmul(po[h * HD:(h + 1) * HD, :], vs[:, jt, h * HD:(h + 1) * HD],
                                     pt[:, jt % 2, h, :], start=(jt == 0), stop=(jt == NT - 1),
                                     tile_position=(0, h * HD))
                for h in range(H):
                    last = nc.tensor.matmul(pd[h * HD:(h + 1) * HD, :], ones[:, 0:HD], pt[:, jt % 2, h, :],
                                            start=(jt == 0), stop=(jt == NT - 1), tile_position=(0, h * HD))
                last.then_inc(s_pv.sem, 1)

            def heads_out(b):
                pe.wait_ge(s_oT.sem, s_oT.at(b, 2 * NC))
                for it in range(NT):
                    last = nc.tensor.matmul(pd[:, it * H:(it + 1) * H], dT[:, it * P:(it + 1) * P], headsel[:, :],
                                            start=True, stop=True)
                last.then_inc(s_dn.sem, 1)
                dst = s_room(b, "on")
                for it in range(NT):
                    last = nc.tensor.transpose(dst[:, it * P:(it + 1) * P], oT[:, it * P:(it + 1) * P], ident[:, :])
                last.then_inc(s_full.sem, 1)

            def projection(b):
                dst = s_room(b, "onT")
                pe.wait_ge(f_dve.sem, f_dve.at(b, SF.emptied(SF.index("on"))))
                for it in range(NT):
                    last = nc.tensor.transpose(dst[:, it * P:(it + 1) * P], on[:, it, :], ident[:, :])
                last.then_inc(s_full.sem, 1)
                dst = s_room(b, "proj")
                pe.wait_ge(f_act.sem, f_act.at(b, SF.emptied(SF.index("onT"))))
                for it in range(NT):
                    last = nc.tensor.matmul(dst[:, it * P:(it + 1) * P], oT[:, it * P:(it + 1) * P], wos[:, :],
                                            start=True, stop=True)
                last.then_inc(s_full.sem, 1)

            def body(b1, b0):
                if b0 is not None:
                    first_mlp(b0)
                if b1 is not None:
                    turn_x1(b1)
                if b0 is not None:
                    node_top(b0, 0)
                if b1 is not None:
                    queries_or_keys(b1, 0, wqs)
                if b0 is not None:
                    f1_rows(b0, 0, [wa1[:, k, :] for k in range(FK)], [r1T[:, k, :] for k in range(FK)])
                if b1 is not None:
                    queries_or_keys(b1, 1, wks)
                    values(b1)
                if b0 is not None:
                    att1(b0, 0, AHEAD * NT)
                if b1 is not None:
                    pe.wait_ge(s_stq.sem, s_stq.at(b1, 16 * 3 * H))
                    pe.wait_ge(s_stk.sem, s_stk.at(b1, 16 * 3 * H))
                for n in range(H * NT):
                    if b1 is not None:
                        row_scores(b1, n)
                    if b0 is not None:
                        att1(b0, att1_through(n - 1), att1_through(n))
                if b1 is not None:
                    turn_max(b1)
                    pe.wait_ge(s_mdma.sem, s_mdma.at(b1, 16))
                for s in range(NC * NT):
                    if b1 is not None:
                        scores(b1, s)
                        if s:
                            products(b1, s - 1)
                    if b0 is not None:
                        if s == Z_AT:
                            turn_z(b0, 0, FK)
                        if s == Z_AT + 1:
                            turn_z(b0, FK, FK * NC)
                        if s == R2_AT:
                            second_mlp(b0)
                        if s == H2_AT:
                            second_h(b0)
                        if s == F2_AT:
                            node_top(b0, 1)
                            f1_rows(b0, 1, [wh1[:, :]], [r2T[:, :]])
                            mean_h(b0)
                        if s >= ATT2_AT:
                            att2(b0, s - ATT2_AT)
                if b1 is not None:
                    products(b1, NC * NT - 1)
                if b0 is not None:
                    turn_r2(b0)
                if b1 is not None:
                    heads_out(b1)
                    projection(b1)

            body(None, 0)
            with pe.Fori(0, B - 1) as b:
                body(b, b + 1)
            body(B - 1, None)


def kernel(x, adj, L0_gnn_mlp1_w, L0_gnn_mlp1_b, L0_gnn_mlp2_w, L0_gnn_mlp2_b, L0_gnn_W_fc, L0_gnn_a_fc,
           L0_gnn_W_hand, L0_gnn_a_hand, L1_gnn_wq, L1_gnn_bq, L1_gnn_wk, L1_gnn_bk, L1_gnn_wv, L1_gnn_bv,
           L1_gnn_wo, L1_gnn_bo):
    import numpy as np
    import concourse.bacc as bacc
    from concourse.bass_utils import run_bass_kernel_spmd

    def rows(a):
        return np.tile(np.asarray(a)[None, :], (P, 1))

    def columns(a):
        return np.asarray(a).reshape(-1, P).T

    def turned(a):
        return np.asarray(a).T

    given = [
        ("x", x), ("adj", adj), ("w1", L0_gnn_mlp1_w), ("b1", columns(L0_gnn_mlp1_b)), ("w2", L0_gnn_mlp2_w),
        ("b2", L0_gnn_mlp2_b), ("wfc", L0_gnn_W_fc), ("wfcT", turned(L0_gnn_W_fc)),
        ("afc", np.asarray(L0_gnn_a_fc).reshape(2, -1, P).transpose(2, 1, 0)), ("wh", L0_gnn_W_hand), ("whT", turned(L0_gnn_W_hand)),
        ("ah", columns(L0_gnn_a_hand)), ("wqT", turned(L1_gnn_wq)), ("bq", L1_gnn_bq),
        ("wkT", turned(L1_gnn_wk)), ("bk", L1_gnn_bk), ("wvT", turned(L1_gnn_wv)), ("bv", rows(L1_gnn_bv)),
        ("woT", turned(L1_gnn_wo)), ("bo", rows(L1_gnn_bo)), ("eye", np.eye(P, dtype=np.float32)),
    ]
    nc = bacc.Bacc("TRN2", target_bir_lowering=False, num_devices=1)
    arrays, args = {}, []
    for name, a in given:
        a = np.ascontiguousarray(a)
        arrays[f"in_{name}"] = a
        args.append(nc.dram_tensor(f"in_{name}", a.shape, mybir.dt.from_np(a.dtype), kind="ExternalInput").ap())
    shape = arrays["in_x"].shape
    args.append(nc.dram_tensor("out_y", shape, F32, kind="ExternalOutput").ap())
    build(nc, *args)
    r = run_bass_kernel_spmd(nc, [arrays], core_ids=[0])
    return r.results[0]["out_y"]
```

```python
from contextlib import ExitStack

import concourse.bass as bass
from concourse import mybir

ALU = mybir.AluOpType
ACT = mybir.ActivationFunctionType
AX = mybir.AxisListType
F32 = mybir.dt.float32
F16 = mybir.dt.float16
BF16 = mybir.dt.bfloat16
I32 = mybir.dt.int32
U8 = mybir.dt.uint8

P = 128
BANK = 512
ALPHA = 0.2
R_TOP = 75.0
MASKED = -1.0e30
LEAST = -60000.0
TINY = 1.0e-30
EPS = 1.0e-5


class Signal:

    def __init__(self, ctx, nc, name, per, first=0):
        self.sem, self.per, self.first = ctx.enter_context(nc.semaphore(name)), per, first

    def at(self, b, n):
        return b * self.per + (n + self.first)


class Fills:

    def __init__(self, order):
        self.fills, self.reader, self.nth, self.banks = [], [], [], []
        for name, count, reader, *banks in order:
            for _ in range(count):
                k = sum(f[0] == name for f in self.fills)
                self.fills.append((name, k))
                self.nth.append(self.reader.count(reader))
                self.reader.append(reader)
                self.banks.append(banks[k % len(banks)] if banks else (len(self.banks) % 2,))
        self.total = len(self.reader)

    def before(self, n):
        found = {}
        for bank in self.banks[n]:
            held = [m for m in range(self.total) if bank in self.banks[m]]
            earlier = [m for m in held if m < n]
            m = earlier[-1] if earlier else held[-1]
            found[self.reader[m]] = max(found.get(self.reader[m], 0), self.emptied(m) if earlier else 0)
        return found

    def index(self, name, k=0):
        return self.fills.index((name, k))

    def emptied(self, n):
        return self.nth[n] + 1

    def count(self, reader):
        return self.reader.count(reader)


def build(nc, x, adj, w1, b1, w2, b2, wfc, wfcT, afc, wh, whT, ah, wqT, bq, wkT, bk, wvT, bv, woT, bo, eye, out):
    B, N, D = x.shape
    NT = N // P
    NC = N // BANK
    TC = BANK // P
    F = w1.shape[1]
    FK = F // P
    H = 4
    HD = D // H
    GW = F + 1
    HW = D + 1
    SCALE = float(HD) ** -0.5
    KS = 3 * HD
    UNITS = NT * H
    assert D == P and FK == 2 and NC == 2

    XF = Fills([("xT", NC, "act"), ("r1", FK * NC, "act"), ("h", NT, "act"), ("top1", 1, "dve"),
                ("f1", NC, "dve"), ("att1", NT, "act"), ("zT", FK * NC, "dve"), ("r2", NC, "act"),
                ("h2", NT // 2, "act"), ("hm", 1, "dve"), ("top2", 1, "dve"), ("f12", NC, "dve"), ("r2n", NC, "act"),
                ("att2", NT // 2, "dve")])
    LEAD = 2
    LOW, HIGH = (0, 1), (2, 3)
    TURNED = [("turned", NC, "act", (2,), (3,), (4,))]
    SF = Fills([("x1T", 1, "act", LOW), ("qk", 2, "dve", HIGH, LOW), ("v", 1, "dve", HIGH), ("score", LEAD, "dve", LOW)]
               + ([("score", 1, "dve", LOW)] + TURNED) * (UNITS - LEAD) + TURNED * LEAD
               + [("on", 1, "dve", HIGH), ("onT", 1, "act", LOW), ("proj", 1, "dve", HIGH)])

    AHEAD = 2
    ATT1_STEP = 6
    Z0_AT, Z1_AT = 6, 9
    Z_AT = 13
    R2_AT = 14
    H2_AT = 15
    F2_AT = 16
    R2N_AT = 20
    P2_STEP = 2
    ATT2_AT = 20
    ATT2_STEP = 8
    OT_AT = 19

    def att1_through(u):
        return min(AHEAD * NT + (u + 1) * ATT1_STEP, NT * NT)

    def att2_through(u):
        n = max(u - ATT2_AT + 1, 0)
        return min(n * P2_STEP if n * P2_STEP <= NT else NT + (n - NT // P2_STEP) * ATT2_STEP, NT * NT)

    def p2_tiles(n):
        return range(max(n, 0) * P2_STEP, min((n + 1) * P2_STEP, NT))

    LN_VAR = NT + 7
    LN_ALL = LN_VAR + 4 + NT
    NS = 4
    NR = 5

    def kept_in(n):
        it, h = n // H, n % H
        k = it // 2 * H + h
        return k % NR, it % 2, (k - NR) // H

    with ExitStack() as ctx:
        def sb(name, shape, dt=F32):
            return ctx.enter_context(nc.sbuf_tensor(name, shape, dt))

        def ps(name, shape, dt=F32):
            return ctx.enter_context(nc.psum_tensor(name, shape, dt))

        def signal(name, per=1, first=0):
            return Signal(ctx, nc, name, per, first)

        ident = sb("ident", [P, P])
        identb = sb("identb", [P, P], BF16)
        ones = sb("ones", [P, P])
        w1s = sb("w1s", [P, F])
        w2s = sb("w2s", [P, FK, D])
        wfx = sb("wfx", [P, FK, GW])
        wa1 = sb("wa1", [P, FK, P])
        whx = sb("whx", [P, HW])
        wh1 = sb("wh1", [P, P])
        afs = sb("afs", [P, FK, 2])
        ahs = sb("ahs", [P, 2])
        b1s = sb("b1s", [P, FK])
        b2s = sb("b2s", [P, 1])
        wqs, wks, wvs, wos = (sb(n, [P, D]) for n in ("wqs", "wks", "wvs", "wos"))
        bqs, bks = sb("bqs", [P, 1]), sb("bks", [P, 1])
        bvs, bos = sb("bvs", [P, D]), sb("bos", [P, D])
        mask = sb("mask", [P, NT, N], BF16)
        maskT = sb("maskT", [P, NT, N], U8)
        rowtop = sb("rowtop", [P, NT])
        dead = sb("dead", [P, NT])
        half = sb("half", [P, NT])
        minus1 = sb("minus1", [P, 1])
        xin = sb("xin", [P, NT, D])
        r1T = sb("r1T", [P, FK, N])
        hx = sb("hx", [P, NT, GW + 1])
        r2T = sb("r2T", [P, N])
        xT = r2T
        r2sum = sb("r2sum", [P, NC])
        h2x = sb("h2x", [P, NT, HW + 1])
        r2bc = sb("r2bc", [P, P])
        hmean = sb("hmean", [P, D])
        f2top = sb("f2top", [P, 1])
        diag = sb("diag", [P, P])
        top = sb("top", [P, 3])
        uv = sb("uv", [P, 2, NT])
        nv = sb("nv", [P, NT])
        rrep = sb("rrep", [P, N])
        pw = sb("pw", [P, NT, N])
        rden = sb("rden", [P, NT])
        nrden = sb("nrden", [P, NT])
        att = sb("att", [P, NT, F])
        el = sb("el", [P, NT, F])
        xh = el[:, NT // 2:NT, :].rearrange("p t f -> p (t f)").rearrange("p (t f) -> p t f", t=NT)
        x2, xr = (att[:, g * NT // 2:(g + 1) * NT // 2, :].rearrange("p t f -> p (t f)").rearrange("p (t f) -> p t f", t=NT)
                  for g in range(2))
        e2 = el[:, 0:NT // 2, :].rearrange("p t f -> p (t f)").rearrange("p (t f) -> p t f", t=NT)
        bn = sb("bn", [P, NT, 6])
        stat = sb("stat", [P, 10, NT])
        x1 = sb("x1", [P, NT, D])
        x1T = sb("x1T", [P, N])
        qst = sb("qst", [KS, H, N], F16)
        kst = sb("kst", [KS, H, N], F16)
        vs = sb("vs", [P, NT, D])
        sm = sb("sm", [P, NS, N])
        mx = sb("mx", [P, UNITS])
        nb = sb("nb", [P, UNITS])
        den = sb("den", [P, UNITS])
        pt = sb("pt", [P, NR, 2, N])
        qp, kp = (pt[:, NR - 1, n, :].bitcast(F16).rearrange("p (a c) -> p a c", a=2) for n in range(2))
        oT = x1T
        rdn = sb("rdn", [P, UNITS])
        on = sb("on", [P, NT, D])
        bn2 = sb("bn2", [P, NT, 6])
        stat2 = sb("stat2", [P, 10, NT])
        setup = pt[:, :, :, :].rearrange("p a e c -> p (a e c)")
        assert NR > H and NS > LEAD
        wfTs = setup[:, 0:FK * F].rearrange("p (k f) -> p k f", k=FK)
        whTs = setup[:, FK * F:FK * F + D]
        linked = setup[:, N:N + NT * N // 2].bitcast(BF16).rearrange("p (t j) -> p t j", t=NT)
        assert FK * F + D <= N
        px = [ps(f"px{n}", [P, BANK]) for n in range(2)]
        pss = [ps(f"pss{n}", [P, N]) for n in range(2)]
        pst = ps("pst", [P, BANK])
        po = ps("po", [P, BANK])

        def setup_bank(n):
            return pss[n // 2 % 2][:, n % 2 * BANK:(n % 2 + 1) * BANK]

        def pair(name, k=0):
            return pss[SF.banks[SF.index(name, k)][0] // 2][:, :]

        def turned(n, c):
            bank = SF.banks[SF.index("turned", NC * n + c)][0]
            return pst[:, :] if bank == 4 else pss[bank // 2][:, bank % 2 * BANK:(bank % 2 + 1) * BANK]

        s_w = signal("s_w")
        s_adj = signal("s_adj")
        s_const = signal("s_const")
        s_linked = signal("s_linked")
        s_mask = signal("s_mask")
        s_dead = signal("s_dead")
        s_minus = signal("s_minus")
        s_mtr = signal("s_mtr")
        s_mtc = signal("s_mtc")
        s_wa = signal("s_wa")
        s_wac = signal("s_wac")
        s_xin = signal("s_xin", 16)
        s_xh = signal("s_xh", 16)
        x_full = signal("x_full", XF.total)
        x_act = signal("x_act", XF.count("act"), 1)
        x_dve = signal("x_dve", XF.count("dve"), 1)
        s_f2top = signal("s_f2top", 2)
        s_diag = signal("s_diag", 2)
        s_topn = signal("s_topn", 4)
        s_uv = signal("s_uv", 4)
        s_nv = signal("s_nv", 1)
        s_r = signal("s_r", 2 * NC)
        s_p1 = signal("s_p1", NT)
        s_over = signal("s_over", NT)
        s_p2 = signal("s_p2", NT)
        s_rden = signal("s_rden", 2 * NT)
        s_min = signal("s_min", 1)
        s_e1 = signal("s_e1", 3)
        s_e2 = signal("s_e2", 3)
        s_z = signal("s_z", 3)
        s_bc = signal("s_bc", 2)
        s_den2 = signal("s_den2", 2 * (NT // 2))
        s_x2 = signal("s_x2", NT)
        s_y = signal("s_y", 2, 1)
        s_ln = signal("s_ln", LN_ALL)
        s_pow = signal("s_pow", 1)
        s_full = signal("s_full", SF.total)
        f_act = signal("f_act", SF.count("act"), 1)
        f_dve = signal("f_dve", SF.count("dve"), 1)
        s_hi = signal("s_hi", 2)
        s_stack = [signal(f"s_stack{h}", 16 * 4) for h in range(H)]
        s_go = signal("s_go", UNITS)
        s_nb = signal("s_nb", UNITS)
        s_den = signal("s_den", UNITS)
        s_pv = signal("s_pv", NT // 2, 1)
        s_oT = signal("s_oT", NC)
        s_dnr = signal("s_dnr", 2)
        s_y2 = signal("s_y2", 1)
        s_ln2 = signal("s_ln2", LN_VAR + 5)
        s_done = signal("s_done", NT)
        s_pow2 = signal("s_pow2", 1)
        s_out = signal("s_out", 16, 1)

        x_nat = x.rearrange("b (t p) d -> b p t d", p=P)
        o_nat = out.rearrange("b (t p) d -> b p t d", p=P)
        N_W = 18
        CONSTS = 5

        block = ctx.enter_context(nc.Block())

        @block.sync
        def _(sp):
            sp.sem_inc(s_out.sem, 1)
            sp.dma_start(pw[:, :, :].bitcast(I32), adj.rearrange("(t p) j -> p t j", p=P)).then_inc(s_adj.sem, 16)
            for dst, src in (
                (ident[:, :], eye), (w1s[:, :], w1), (b1s[:, :], b1),
                (wfx[:, :, 1:GW], wfc.rearrange("(k p) f -> p k f", p=P)),
                (wfTs[:, :, :], wfcT.rearrange("(k p) f -> p k f", p=P)),
                (afs[:, :, :], afc),
                (w2s[:, :, :], w2.rearrange("(k p) f -> p k f", p=P)),
                (b2s[:, :], b2.rearrange("(p o) -> p o", o=1)),
                (whx[:, 1:HW], wh), (whTs[:, :], whT),
                (ahs[:, :], ah),
                (wqs[:, :], wqT), (wks[:, :], wkT), (wvs[:, :], wvT), (wos[:, :], woT),
                (bqs[:, :], bq.rearrange("(p o) -> p o", o=1)), (bks[:, :], bk.rearrange("(p o) -> p o", o=1)),
                (bvs[:, :], bv), (bos[:, :], bo),
            ):
                sp.dma_start(dst, src).then_inc(s_w.sem, 16)

            def load_head(b):
                sp.wait_ge(s_z.sem, s_z.at(b - 1, 2))
                sp.dma_start(xh, x_nat[b]).then_inc(s_xh.sem, 16)

            def load_x(b):
                sp.wait_ge(s_y.sem, s_y.at(b, 0))
                sp.dma_start(xin[:, :, :], x_nat[b]).then_inc(s_xin.sem, 16)

            def stack(b):
                sp.wait_ge(f_dve.sem, f_dve.at(b, SF.emptied(SF.index("qk", 1))))
                for h in range(H):
                    rows = slice(h * HD, (h + 1) * HD)
                    for dst, src in ((qst[0:2 * HD, h, :], qp[rows, :, :]),
                                     (kst[0:2 * HD, h, :], kp[rows, 0:1, :].to_broadcast([HD, 2, N])),
                                     (qst[2 * HD:3 * HD, h, :], qp[rows, 0, :]),
                                     (kst[2 * HD:3 * HD, h, :], kp[rows, 1, :])):
                        sp.dma_start(dst, src).then_inc(s_stack[h].sem, 16)

            def store(b):
                sp.wait_ge(s_done.sem, s_done.at(b, NT))
                sp.dma_start(o_nat[b], on[:, :, :]).then_inc(s_out.sem, 16)

            sp.dma_start(xh, x_nat[0]).then_inc(s_xh.sem, 16)
            load_x(0)
            load_head(1)
            load_x(1)
            stack(0)
            with sp.Fori(0, B - 2) as b:
                load_head(b + 2)
                load_x(b + 2)
                stack(b + 1)
                store(b)
            stack(B - 1)
            store(B - 2)
            store(B - 1)
            sp.wait_ge(s_out.sem, 16 * B + 1)

        @block.gpsimd
        def _(pool):
            for n, (dst, value) in enumerate(((ones[:, :], 1.0), (hx[:, :, GW:GW + 1], 1.0), (h2x[:, :, HW:HW + 1], 1.0),
                                              (half[:, :], -0.5))):
                nc.gpsimd.memset(dst, value).then_inc(s_const.sem, 1)
                pool.wait_ge(s_const.sem, n + 1)
            pool.wait_ge(s_w.sem, 16 * (N_W + 1))
            nc.gpsimd.tensor_copy(identb[:, :], ident[:, :]).then_inc(s_const.sem, 1)
            pool.wait_ge(s_const.sem, CONSTS)

            def power(b, st, ln, done):
                pool.wait_ge(ln.sem, ln.at(b, LN_VAR))
                nc.gpsimd.tensor_tensor(st[:, 3, :], st[:, 2, :], half[:, :], ALU.pow).then_inc(done.sem, 1)

            def biased(b):
                pool.wait_ge(f_dve.sem, f_dve.at(b, SF.emptied(SF.index("proj"))))
                nc.gpsimd.tensor_tensor(on[:, :, :], on[:, :, :], bos[:, :].unsqueeze(1).to_broadcast([P, NT, D]),
                                        ALU.add).then_inc(s_y2.sem, 1)

            power(0, stat, s_ln, s_pow)
            with pool.Fori(0, B - 1) as b:
                power(b + 1, stat, s_ln, s_pow)
                biased(b)
                power(b, stat2, s_ln2, s_pow2)
            biased(B - 1)
            power(B - 1, stat2, s_ln2, s_pow2)

        @block.scalar
        def _(act):
            act.sem_inc(x_act.sem, 1)
            act.sem_inc(f_act.sem, 1)
            act.wait_ge(s_w.sem, 16 * (N_W + 1))
            act.wait_ge(s_const.sem, CONSTS)
            act.wait_ge(s_minus.sem, 1)

            def x_filled(b, name, k=0):
                act.wait_ge(x_full.sem, x_full.at(b, XF.index(name, k) + 1))

            def elus(b, n, part, sign):
                nc.scalar.activation(part, part, ACT.Exp, scale=sign).then_inc(s_e1.sem, 1)
                act.wait_ge(s_e1.sem, s_e1.at(b, n + 1))
                nc.scalar.activation(part, part, ACT.Exp, bias=minus1[:, :]).then_inc(s_e2.sem, 1)

            def gat0_row(b, it):
                src = px[XF.index("att1", it) % 2]
                act.wait_ge(s_rden.sem, s_rden.at(b, 2 * it + 2))
                nc.scalar.activation(att[:, it, :], src[:, 0:F], ACT.Relu, scale=rden[:, it:it + 1])
                nc.scalar.activation(el[:, it, :], src[:, 0:F], ACT.Relu,
                                     scale=nrden[:, it:it + 1]).then_inc(x_act.sem, 1)
                if it % (NT // 2) == NT // 2 - 1:
                    g = it // (NT // 2)
                    act.wait_ge(x_act.sem, x_act.at(b, XF.emptied(XF.index("att1", it))))
                    elus(b, g, el[:, g * NT // 2:(g + 1) * NT // 2, :], -1.0)

            def exponentials(b, n):
                act.wait_ge(s_nb.sem, s_nb.at(b, n + 1))
                nc.scalar.activation(sm[:, n % NS, :], sm[:, n % NS, :], ACT.Exp, bias=nb[:, n:n + 1], scale=SCALE,
                                     accum_out=den[:, n:n + 1]).then_inc(s_den.sem, 1)

            def powers(b, n, hxt):
                act.wait_ge(s_topn.sem, s_topn.at(b, 2 * n + 2))
                if n == 1:
                    act.wait_ge(s_p1.sem, s_p1.at(b, NT))
                nc.scalar.activation(uv[:, 0, :], hxt[:, :, 0], ACT.Exp, bias=top[:, 1:2]).then_inc(s_uv.sem, 1)
                nc.scalar.activation(uv[:, 1, :], hxt[:, :, 0], ACT.Exp, bias=top[:, 2:3],
                                     scale=ALPHA).then_inc(s_uv.sem, 1)

            def factors(b, n):
                for c in range(NC):
                    k = XF.emptied(XF.index(("f1", "f12")[n], c))
                    act.wait_ge(x_dve.sem, x_dve.at(b, k))
                    nc.scalar.activation(rrep[:, c * BANK:(c + 1) * BANK], rrep[:, c * BANK:(c + 1) * BANK],
                                         ACT.Exp, scale=1.0 - ALPHA).then_inc(s_r.sem, 1)

            def keep_turned(b, n):
                buffer, tile_of_pair, pair_before = kept_in(n)
                act.wait_ge(s_pv.sem, s_pv.at(b, max(pair_before + 1, 0)))
                for c in range(NC):
                    act.wait_ge(s_full.sem, s_full.at(b, SF.index("turned", NC * n + c) + 1))
                    nc.scalar.activation(pt[:, buffer, tile_of_pair, c * BANK:(c + 1) * BANK], turned(n, c),
                                         ACT.Copy).then_inc(f_act.sem, 1)

            def over(b, jt):
                nc.scalar.activation(pw[:, jt, :], rrep[:, :], ACT.Relu, bias=nv[:, jt:jt + 1],
                                     scale=uv[:, 0, jt:jt + 1]).then_inc(s_over.sem, 1)

            def high_half(b, n, bias):
                m = SF.index("qk", n)
                act.wait_ge(s_full.sem, s_full.at(b, m + 1))
                nc.scalar.activation((qp, kp)[n][:, 0, :], pair("qk", n), ACT.Identity,
                                     bias=bias[:, :]).then_inc(s_hi.sem, 1)

            def join(b1, b0, bh):
                if bh is not None:
                    for c in range(NC):
                        x_filled(bh, "xT", c)
                        nc.scalar.activation(xT[:, c * BANK:(c + 1) * BANK], px[XF.index("xT", c) % 2][:, :],
                                             ACT.Copy).then_inc(x_act.sem, 1)
                if b0 is not None:
                    act.wait_ge(s_min.sem, s_min.at(b0, 1))
                    elus(b0, 2, el[:, 0:NT // 2, :], 1.0)
                for n in range(FK * NC):
                    if bh is not None:
                        k, c = n // NC, n % NC
                        x_filled(bh, "r1", n)
                        nc.scalar.activation(r1T[:, k, c * BANK:(c + 1) * BANK], px[XF.index("r1", n) % 2][:, :],
                                             ACT.Relu, bias=b1s[:, k:k + 1]).then_inc(x_act.sem, 1)
                    if b1 is not None and n == FK * NC // 2 - 1:
                        act.wait_ge(s_full.sem, s_full.at(b1, SF.index("onT") + 1))
                        nc.scalar.activation(oT[:, :], pair("onT"), ACT.Copy).then_inc(f_act.sem, 1)
                if bh is not None:
                    for jt in range(NT):
                        x_filled(bh, "h", jt)
                        nc.scalar.activation(hx[:, jt, 0:GW], px[XF.index("h", jt) % 2][:, 0:GW],
                                             ACT.Copy).then_inc(x_act.sem, 1)
                if b0 is not None:
                    act.wait_ge(s_full.sem, s_full.at(b0, SF.index("x1T") + 1))
                    nc.scalar.activation(x1T[:, :], pair("x1T"), ACT.Copy).then_inc(f_act.sem, 1)
                if bh is not None:
                    powers(bh, 0, hx)
                if b0 is not None:
                    high_half(b0, 0, bqs)
                if bh is not None:
                    factors(bh, 0)
                if b0 is not None:
                    high_half(b0, 1, bks)
                if b1 is not None:
                    act.wait_ge(s_ln2.sem, s_ln2.at(b1, LN_VAR + 5))
                    for it in range(NT):
                        nc.scalar.activation(on[:, it, :], on[:, it, :], ACT.Identity, bias=stat2[:, 9, it:it + 1],
                                             scale=stat2[:, 7, it:it + 1]).then_inc(s_done.sem, 1)

            def middle(b1, b0):
                if b1 is not None:
                    exponentials(b1, 0)
                if b0 is not None:
                    for it in range(AHEAD):
                        gat0_row(b0, it)
                for u in range(UNITS):
                    if b1 is not None and u:
                        keep_turned(b1, u - 1)
                    if b0 is not None:
                        for it in range(att1_through(u - 2) // NT if u else NT, att1_through(u - 1) // NT):
                            gat0_row(b0, it)
                        if u == R2N_AT:
                            for c in range(NC):
                                x_filled(b0, "r2n", c)
                                nc.scalar.activation(xr[:, c * TC:(c + 1) * TC, :], px[XF.index("r2n", c) % 2][:, :]
                                                     .rearrange("p (t f) -> p t f", f=D), ACT.Copy).then_inc(x_act.sem, 1)
                        if u == R2_AT:
                            for c in range(NC):
                                x_filled(b0, "r2", c)
                                nc.scalar.activation(r2T[:, c * BANK:(c + 1) * BANK], px[XF.index("r2", c) % 2][:, :],
                                                     ACT.Relu, bias=b2s[:, :],
                                                     accum_out=r2sum[:, c:c + 1]).then_inc(x_act.sem, 1)
                        if u == H2_AT:
                            for n in range(NT // 2):
                                x_filled(b0, "h2", n)
                                nc.scalar.activation(
                                    h2x[:, 2 * n:2 * n + 2, 0:HW],
                                    px[XF.index("h2", n) % 2][:, 0:2 * HW].rearrange("p (t f) -> p t f", t=2),
                                    ACT.Copy).then_inc(x_act.sem, 1)
                        if u == F2_AT:
                            powers(b0, 1, h2x)
                            act.wait_ge(s_uv.sem, s_uv.at(b0, 4))
                            nc.scalar.activation(nv[:, :], uv[:, 1, :], ACT.Copy, scale=-1.0).then_inc(s_nv.sem, 1)
                            factors(b0, 1)
                            act.wait_ge(s_nv.sem, s_nv.at(b0, 1))
                            act.wait_ge(s_r.sem, s_r.at(b0, 2 * NC))
                        for jt in p2_tiles(u - F2_AT - 1) if u > F2_AT else ():
                            over(b0, jt)
                    if b1 is not None and u + 1 < UNITS:
                        exponentials(b1, u + 1)
                if b1 is not None:
                    keep_turned(b1, UNITS - 1)

            join(None, None, 0)
            for jt in range(NT):
                act.wait_ge(s_mtr.sem, jt + 1)
                nc.scalar.activation(maskT[:, jt, :], setup_bank(jt).bitcast(BF16), ACT.Copy).then_inc(s_mtc.sem, 1)
            middle(None, 0)
            join(None, 0, 1)
            with act.Fori(0, B - 2) as b:
                middle(b, b + 1)
                join(b, b + 1, b + 2)
            middle(B - 2, B - 1)
            join(B - 2, B - 1, None)
            middle(B - 1, None)
            join(B - 1, None, None)

        @block.vector
        def _(dve):
            dve.sem_inc(x_dve.sem, 1)
            dve.sem_inc(f_dve.sem, 1)
            dve.sem_inc(s_y.sem, 1)
            nc.vector.memset(minus1[:, :], -1.0).then_inc(s_minus.sem, 1)
            dve.wait_ge(s_adj.sem, 16)
            for it in range(NT):
                a = pw[:, it, :].bitcast(I32)
                nc.vector.tensor_scalar(linked[:, it, :], a, 0, None, ALU.is_gt).then_inc(s_linked.sem, 1)
                nc.vector.tensor_scalar(mask[:, it, :], a, 0, MASKED, ALU.is_equal, ALU.mult).then_inc(s_mask.sem, 1)
            dve.wait_ge(s_wa.sem, FK + 1)
            for k in range(FK):
                nc.vector.tensor_copy(wfx[:, k, 0:1], po[:, 2 * k + 1:2 * k + 2]).then_inc(s_wac.sem, 1)
                nc.vector.tensor_scalar(wa1[:, k, :], ones[:, :], po[:, 2 * k:2 * k + 1], None,
                                        ALU.mult).then_inc(s_wac.sem, 1)
            nc.vector.tensor_copy(whx[:, 0:1], po[:, 5:6]).then_inc(s_wac.sem, 1)
            nc.vector.tensor_scalar(wh1[:, :], ones[:, :], po[:, 4:5], None, ALU.mult).then_inc(s_wac.sem, 1)
            for it in range(NT):
                dve.wait_ge(s_linked.sem, it + 1)
                nc.vector.reduce_max(rowtop[:, it:it + 1], linked[:, it, :], axis=AX.X).then_inc(s_dead.sem, 1)
            dve.wait_ge(s_dead.sem, NT)
            nc.vector.tensor_scalar(dead[:, :], rowtop[:, :], 1.0, None, ALU.is_lt).then_inc(s_dead.sem, 1)
            dve.wait_ge(s_dead.sem, NT + 1)

            def x_filled(b, name, k=0):
                dve.wait_ge(x_full.sem, x_full.at(b, XF.index(name, k) + 1))
                return px[XF.index(name, k) % 2]

            def diagonal(b, n, hxt):
                done = XF.emptied(XF.index(("h", "h2")[n], (NT, NT // 2)[n] - 1))
                dve.wait_ge(x_act.sem, x_act.at(b, done))
                nc.vector.reduce_max(f2top[:, :], hxt[:, :, 0], axis=AX.X).then_inc(s_f2top.sem, 1)
                dve.wait_ge(s_f2top.sem, s_f2top.at(b, n + 1))
                nc.vector.tensor_scalar(diag[:, :], ident[:, :], f2top[:, :], None, ALU.mult).then_inc(s_diag.sem, 1)

            def find_top(b, n):
                src = x_filled(b, ("top1", "top2")[n])
                nc.vector.reduce_max(top[:, 0:1], src[:, 0:P], axis=AX.X).then_inc(x_dve.sem, 1)
                dve.wait_ge(x_dve.sem, x_dve.at(b, XF.emptied(XF.index(("top1", "top2")[n]))))
                nc.vector.tensor_scalar(top[:, 1:2], top[:, 0:1], -1.0, None, ALU.mult).then_inc(s_topn.sem, 1)
                nc.vector.tensor_scalar(top[:, 2:3], top[:, 0:1], -ALPHA, None, ALU.mult).then_inc(s_topn.sem, 1)

            def f1_plus_top(b, n, c):
                src = x_filled(b, ("f1", "f12")[n], c)
                nc.vector.tensor_scalar(rrep[:, c * BANK:(c + 1) * BANK], src[:, :], top[:, 0:1], R_TOP,
                                        ALU.add, ALU.min).then_inc(x_dve.sem, 1)

            def variance(b, ln, y, bn, st):
                for it in range(NT):
                    nc.vector.bn_stats(bn[:, it, :], y[:, it, :]).then_inc(ln.sem, 1)
                dve.wait_ge(ln.sem, ln.at(b, NT))
                nc.vector.tensor_tensor(st[:, 0, :], bn[:, :, 1], bn[:, :, 4], ALU.add).then_inc(ln.sem, 1)
                nc.vector.tensor_tensor(st[:, 1, :], bn[:, :, 1], bn[:, :, 4], ALU.subtract).then_inc(ln.sem, 1)
                nc.vector.tensor_tensor(st[:, 4, :], bn[:, :, 2], bn[:, :, 5], ALU.add).then_inc(ln.sem, 1)
                dve.wait_ge(ln.sem, ln.at(b, NT + 3))
                nc.vector.tensor_scalar(st[:, 8, :], st[:, 0, :], 0.5, None, ALU.mult).then_inc(ln.sem, 1)
                nc.vector.tensor_scalar(st[:, 5, :], st[:, 4, :], 1.0 / D, EPS, ALU.mult, ALU.add).then_inc(ln.sem, 1)
                nc.vector.scalar_tensor_tensor(st[:, 6, :], st[:, 1, :], 0.25, st[:, 1, :], ALU.mult,
                                               ALU.mult).then_inc(ln.sem, 1)
                dve.wait_ge(ln.sem, ln.at(b, NT + 6))
                nc.vector.tensor_tensor(st[:, 2, :], st[:, 5, :], st[:, 6, :], ALU.add).then_inc(ln.sem, 1)

            def deviation(b, ln, pow_done, st):
                dve.wait_ge(pow_done.sem, pow_done.at(b, 1))
                nc.vector.tensor_tensor(st[:, 4, :], st[:, 3, :], st[:, 3, :], ALU.mult).then_inc(ln.sem, 1)
                dve.wait_ge(ln.sem, ln.at(b, LN_VAR + 1))
                nc.vector.tensor_tensor(st[:, 5, :], st[:, 4, :], st[:, 2, :], ALU.mult).then_inc(ln.sem, 1)
                dve.wait_ge(ln.sem, ln.at(b, LN_VAR + 2))
                nc.vector.tensor_scalar(st[:, 6, :], st[:, 5, :], -0.5, 1.5, ALU.mult, ALU.add).then_inc(ln.sem, 1)
                dve.wait_ge(ln.sem, ln.at(b, LN_VAR + 3))
                nc.vector.tensor_tensor(st[:, 7, :], st[:, 3, :], st[:, 6, :], ALU.mult).then_inc(ln.sem, 1)
                dve.wait_ge(ln.sem, ln.at(b, LN_VAR + 4))

            def norm1(b):
                deviation(b, s_ln, s_pow, stat)
                for it in range(NT):
                    nc.vector.tensor_scalar(x1[:, it, :], x2[:, it, :], stat[:, 8, it:it + 1], stat[:, 7, it:it + 1],
                                            ALU.subtract, ALU.mult).then_inc(s_ln.sem, 1)

            def norm2(b):
                deviation(b, s_ln2, s_pow2, stat2)
                nc.vector.scalar_tensor_tensor(stat2[:, 9, :], stat2[:, 8, :], -1.0, stat2[:, 7, :], ALU.mult,
                                               ALU.mult).then_inc(s_ln2.sem, 1)

            def gat0_weights(b, first, end):
                dve.wait_ge(s_uv.sem, s_uv.at(b, 2))
                dve.wait_ge(s_r.sem, s_r.at(b, NC))
                for jt in range(first, end):
                    nc.vector.tensor_scalar(pw[:, jt, :], rrep[:, :], uv[:, 0, jt:jt + 1], uv[:, 1, jt:jt + 1],
                                            ALU.mult, ALU.max).then_inc(s_p1.sem, 1)

            def gat0_row(b, it):
                src = x_filled(b, "att1", it)
                nc.vector.reciprocal(rden[:, it:it + 1], src[:, F:F + 1]).then_inc(s_rden.sem, 1)
                dve.wait_ge(s_rden.sem, s_rden.at(b, 2 * it + 1))
                nc.vector.tensor_scalar(nrden[:, it:it + 1], rden[:, it:it + 1], -1.0, None,
                                        ALU.mult).then_inc(s_rden.sem, 1)

            def gat0_elu(b, g):
                part = slice(g * NT // 2, (g + 1) * NT // 2)
                dve.wait_ge(s_e2.sem, s_e2.at(b, g + 1))
                nc.vector.tensor_tensor(att[:, part, :], att[:, part, :], el[:, part, :], ALU.add).then_inc(s_z.sem, 1)

            def residual0(b):
                for n in range(FK * NC):
                    k, c = n % FK, n // FK
                    src = x_filled(b, "zT", n)
                    r = r1T[:, k, c * BANK:(c + 1) * BANK]
                    nc.vector.scalar_tensor_tensor(r, src[:, :], -1.0, r, ALU.add, ALU.add).then_inc(x_dve.sem, 1)

            def gat1_mean(b):
                dve.wait_ge(x_act.sem, x_act.at(b, XF.emptied(XF.index("r2", NC - 1))))
                nc.vector.tensor_tensor(r2sum[:, 0:1], r2sum[:, 0:1], r2sum[:, 1:2], ALU.add).then_inc(s_bc.sem, 1)
                dve.wait_ge(s_bc.sem, s_bc.at(b, 1))
                nc.vector.tensor_scalar(r2bc[:, :], ones[:, :], r2sum[:, 0:1], 1.0 / N, ALU.mult,
                                        ALU.mult).then_inc(s_bc.sem, 1)
                diagonal(b, 1, h2x)

            def gat1_factors(b):
                src = x_filled(b, "hm")
                nc.vector.tensor_copy(hmean[:, :], src[:, 0:D]).then_inc(x_dve.sem, 1)
                find_top(b, 1)
                for c in range(NC):
                    f1_plus_top(b, 1, c)

            def gat1_masked(b, jt):
                dve.wait_ge(s_over.sem, s_over.at(b, jt + 1))
                nc.vector.scalar_tensor_tensor(pw[:, jt, :], pw[:, jt, :], uv[:, 1, jt:jt + 1], maskT[:, jt, :],
                                               ALU.add, ALU.mult).then_inc(s_p2.sem, 1)

            def gat1_rows(b, n):
                tt = slice(2 * n, 2 * n + 2)
                src = x_filled(b, "att2", n)[:, 0:2 * HW].rearrange("p (t f) -> p t f", t=2)
                nc.vector.tensor_scalar(rden[:, tt], src[:, :, D], TINY, None, ALU.max).then_inc(s_den2.sem, 1)
                dve.wait_ge(s_den2.sem, s_den2.at(b, 2 * n + 1))
                nc.vector.reciprocal(rden[:, tt], rden[:, tt]).then_inc(s_den2.sem, 1)
                dve.wait_ge(s_den2.sem, s_den2.at(b, 2 * n + 2))
                nc.vector.tensor_tensor(x2[:, tt, :], src[:, :, 0:D], rden[:, tt].unsqueeze(2).to_broadcast([P, 2, D]),
                                        ALU.mult).then_inc(x_dve.sem, 1)
                dve.wait_ge(x_dve.sem, x_dve.at(b, XF.emptied(XF.index("att2", n))))
                for it in range(2 * n, 2 * n + 2):
                    nc.vector.scalar_tensor_tensor(x2[:, it, :], hmean[:, :], dead[:, it:it + 1], x2[:, it, :],
                                                   ALU.mult, ALU.add).then_inc(s_x2.sem, 1)

            def gat1_min(b):
                dve.wait_ge(s_x2.sem, s_x2.at(b, NT))
                nc.vector.tensor_scalar(e2, x2, 0.0, None, ALU.min).then_inc(s_min.sem, 1)

            def residual1(b):
                dve.wait_ge(s_e2.sem, s_e2.at(b, 3))
                nc.vector.scalar_tensor_tensor(x2, x2, 0.0, e2, ALU.max, ALU.add).then_inc(s_z.sem, 1)
                dve.wait_ge(s_z.sem, s_z.at(b, 3))
                dve.wait_ge(s_xin.sem, s_xin.at(b, 16))
                dve.wait_ge(x_act.sem, x_act.at(b, XF.emptied(XF.index("r2n", NC - 1))))
                nc.vector.scalar_tensor_tensor(x2, xr, -1.0, x2, ALU.add, ALU.add).then_inc(s_y.sem, 1)
                dve.wait_ge(s_y.sem, s_y.at(b, 1))
                nc.vector.scalar_tensor_tensor(x2, x2, 0.0, xin[:, :, :], ALU.max, ALU.add).then_inc(s_y.sem, 1)
                dve.wait_ge(s_y.sem, s_y.at(b, 2))

            def low_half(b, n, bias):
                dve.wait_ge(s_hi.sem, s_hi.at(b, n + 1))
                halves = (qp, kp)[n]
                nc.vector.scalar_tensor_tensor(halves[:, 1, :], pair("qk", n), bias[:, :],
                                               halves[:, 0, :], ALU.add, ALU.subtract).then_inc(f_dve.sem, 1)

            def values(b):
                dve.wait_ge(s_full.sem, s_full.at(b, SF.index("v") + 1))
                nc.vector.tensor_tensor(vs[:, :, :], pair("v").rearrange("p (t f) -> p t f", f=D),
                                        bvs[:, :].unsqueeze(1).to_broadcast([P, NT, D]),
                                        ALU.add).then_inc(f_dve.sem, 1)

            def row_max(b, n):
                m = SF.index("score", n)
                if n >= NS:
                    dve.wait_ge(s_full.sem, s_full.at(b, SF.index("turned", NC * (n - NS) + 1) + 1))
                dve.wait_ge(s_full.sem, s_full.at(b, m + 1))
                dve.sem_inc(s_go.sem, 1)
                nc.vector.tensor_tensor_reduce(out=sm[:, n % NS, :], in0=pair("score", n), in1=mask[:, n // H, :],
                                               scale=1.0, scalar=-3.0e38, op0=ALU.add, op1=ALU.max,
                                               accum_out=mx[:, n:n + 1]).then_inc(f_dve.sem, 1)
                dve.wait_ge(f_dve.sem, f_dve.at(b, SF.emptied(m)))
                nc.vector.tensor_scalar(nb[:, n:n + 1], mx[:, n:n + 1], LEAST, -SCALE, ALU.max,
                                        ALU.mult).then_inc(s_nb.sem, 1)

            def accumulated(b, c):
                dve.wait_ge(s_pv.sem, s_pv.at(b, (c + 1) * TC // 2))
                nc.vector.tensor_copy(oT[:, c * BANK:(c + 1) * BANK], po[:, :]).then_inc(s_oT.sem, 1)

            def denominators(b):
                dve.wait_ge(s_den.sem, s_den.at(b, UNITS))
                nc.vector.tensor_scalar(rdn[:, :], den[:, :], TINY, None, ALU.max).then_inc(s_dnr.sem, 1)
                dve.wait_ge(s_dnr.sem, s_dnr.at(b, 1))
                nc.vector.reciprocal(rdn[:, :], rdn[:, :]).then_inc(s_dnr.sem, 1)

            def divided(b):
                dve.wait_ge(s_dnr.sem, s_dnr.at(b, 2))
                dve.wait_ge(s_full.sem, s_full.at(b, SF.index("on") + 1))
                dve.wait_ge(s_out.sem, s_out.at(b, 0))
                nc.vector.tensor_tensor(on[:, :, :].rearrange("p t (h d) -> p t h d", h=H),
                                        pair("on").rearrange("p (t h d) -> p t h d", h=H, d=HD),
                                        rdn[:, :].rearrange("p (t h) -> p t h", h=H).unsqueeze(3)
                                        .to_broadcast([P, NT, H, HD]), ALU.mult).then_inc(f_dve.sem, 1)

            def residual2(b):
                dve.wait_ge(s_full.sem, s_full.at(b, SF.index("proj") + 1))
                nc.vector.tensor_tensor(on[:, :, :], pair("proj").rearrange("p (t f) -> p t f", f=D),
                                        x1[:, :, :], ALU.add).then_inc(f_dve.sem, 1)

            def join(b1, b0, bh):
                if b1 is not None:
                    denominators(b1)
                    accumulated(b1, 1)
                if b0 is not None:
                    for n in range(att2_through(UNITS - 2) // (2 * NT), NT // 2):
                        gat1_rows(b0, n)
                    gat1_min(b0)
                if b1 is not None:
                    divided(b1)
                if b0 is not None:
                    residual1(b0)
                    variance(b0, s_ln, x2, bn, stat)
                if b1 is not None:
                    residual2(b1)
                if b0 is not None:
                    norm1(b0)
                if bh is not None:
                    diagonal(bh, 0, hx)
                    find_top(bh, 0)
                if b1 is not None:
                    dve.wait_ge(s_y2.sem, s_y2.at(b1, 1))
                    variance(b1, s_ln2, on, bn2, stat2)
                if bh is not None:
                    f1_plus_top(bh, 0, 0)
                if b0 is not None:
                    low_half(b0, 0, bqs)
                if bh is not None:
                    f1_plus_top(bh, 0, 1)
                    gat0_weights(bh, 0, NT // 2)
                if b1 is not None:
                    norm2(b1)
                if b0 is not None:
                    low_half(b0, 1, bks)
                if bh is not None:
                    gat0_weights(bh, NT // 2, NT)
                if b0 is not None:
                    values(b0)

            def middle(b1, b0):
                if b1 is not None:
                    for n in range(LEAD):
                        row_max(b1, n)
                if b0 is not None:
                    for it in range(AHEAD):
                        gat0_row(b0, it)
                for u in range(UNITS):
                    if b0 is not None:
                        for it in range(att1_through(u - 2) // NT if u else NT, att1_through(u - 1) // NT):
                            gat0_row(b0, it)
                        if u == F2_AT:
                            gat1_mean(b0)
                    if b1 is not None:
                        if u + LEAD < UNITS:
                            row_max(b1, u + LEAD)
                        if u == OT_AT:
                            accumulated(b1, 0)
                    if b0 is not None:
                        if u in (Z0_AT, Z1_AT):
                            gat0_elu(b0, int(u == Z1_AT))
                        if u == Z_AT:
                            residual0(b0)
                        if u == F2_AT:
                            gat1_factors(b0)
                        for jt in p2_tiles(u - F2_AT - 2) if u > F2_AT + 1 else ():
                            gat1_masked(b0, jt)
                        for n in range(att2_through(u - 2) // (2 * NT), att2_through(u - 1) // (2 * NT)):
                            gat1_rows(b0, n)

            dve.wait_ge(s_w.sem, 16 * (N_W + 1))
            dve.wait_ge(s_const.sem, CONSTS)
            dve.wait_ge(s_wac.sem, 2 * FK + 2)
            dve.wait_ge(s_minus.sem, 1)
            dve.wait_ge(s_mask.sem, NT)
            join(None, None, 0)
            dve.wait_ge(s_mtc.sem, NT)
            middle(None, 0)
            join(None, 0, 1)
            with dve.Fori(0, B - 2) as b:
                middle(b, b + 1)
                join(b, b + 1, b + 2)
            middle(B - 2, B - 1)
            join(B - 2, B - 1, None)
            middle(B - 1, None)
            join(B - 1, None, None)

        @block.tensor
        def _(pe):
            pe.sem_inc(s_pv.sem, 1)
            pe.wait_ge(s_w.sem, 16 * (N_W + 1))
            pe.wait_ge(s_const.sem, CONSTS)
            for k in range(FK):
                for f in range(FK):
                    last = nc.tensor.matmul(po[:, 2 * k:2 * k + 2], wfTs[:, f, k * P:(k + 1) * P], afs[:, f, :],
                                            start=(f == 0), stop=(f == FK - 1))
                last.then_inc(s_wa.sem, 1)
            nc.tensor.matmul(po[:, 4:6], whTs[:, :], ahs[:, :], start=True, stop=True).then_inc(s_wa.sem, 1)
            pe.wait_ge(s_wac.sem, 2 * FK + 2)

            def x_room(b, name, k=0):
                n = XF.index(name, k)
                if n < 2:
                    pe.wait_ge(x_dve.sem, x_dve.at(b, 0))
                elif XF.reader[n - 2] == "act":
                    pe.wait_ge(x_act.sem, x_act.at(b, XF.emptied(n - 2)))
                else:
                    pe.wait_ge(x_dve.sem, x_dve.at(b, XF.emptied(n - 2)))
                return px[n % 2]

            def s_room(b, name, k=0):
                for reader, emptied in SF.before(SF.index(name, k)).items():
                    last = {"act": f_act, "dve": f_dve}[reader]
                    pe.wait_ge(last.sem, last.at(b, emptied))

            def emptied_act(b, name, k=0):
                pe.wait_ge(x_act.sem, x_act.at(b, XF.emptied(XF.index(name, k))))

            def node_top(b, n):
                dst = x_room(b, ("top1", "top2")[n])
                pe.wait_ge(s_diag.sem, s_diag.at(b, n + 1))
                nc.tensor.matmul(dst[:, 0:P], ones[:, :], diag[:, :], start=True, stop=True).then_inc(x_full.sem, 1)

            def f1_rows(b, n, w, src, c):
                dst = x_room(b, ("f1", "f12")[n], c)
                for k in range(len(w)):
                    last = nc.tensor.matmul(dst[:, :], w[k], src[k][:, c * BANK:(c + 1) * BANK],
                                            start=(k == 0), stop=(k == len(w) - 1))
                last.then_inc(x_full.sem, 1)

            def turn_x(b):
                pe.wait_ge(s_xh.sem, s_xh.at(b, 16))
                for c in range(NC):
                    dst = x_room(b, "xT", c)
                    for t in range(TC):
                        last = nc.tensor.transpose(dst[:, t * P:(t + 1) * P], xh[:, c * TC + t, :], ident[:, :])
                    last.then_inc(x_full.sem, 1)

            def first_mlp(b, k):
                for c in range(NC):
                    dst = x_room(b, "r1", k * NC + c)
                    emptied_act(b, "xT", c)
                    nc.tensor.matmul(dst[:, :], w1s[:, k * P:(k + 1) * P], xT[:, c * BANK:(c + 1) * BANK],
                                     start=True, stop=True).then_inc(x_full.sem, 1)

            def first_h(b):
                emptied_act(b, "r1", FK * NC - 1)
                for jt in range(NT):
                    dst = x_room(b, "h", jt)
                    for k in range(FK):
                        last = nc.tensor.matmul(dst[:, 0:GW], r1T[:, k, jt * P:(jt + 1) * P], wfx[:, k, :],
                                                start=(k == 0), stop=(k == FK - 1))
                    last.then_inc(x_full.sem, 1)

            def att1(b, first, end):
                for m in range(first, end):
                    it, jt = m // NT, m % NT
                    if jt == 0:
                        x_room(b, "att1", it)
                    if it == 0:
                        pe.wait_ge(s_p1.sem, s_p1.at(b, jt + 1))
                    last = nc.tensor.matmul(px[XF.index("att1", it) % 2][:, 0:GW], pw[:, jt, it * P:(it + 1) * P],
                                            hx[:, jt, 1:GW + 1], start=(jt == 0), stop=(jt == NT - 1))
                    if jt == NT - 1:
                        last.then_inc(x_full.sem, 1)

            def turn_z(b, first, end):
                for n in range(first, end):
                    k, c = n % FK, n // FK
                    dst = x_room(b, "zT", n)
                    pe.wait_ge(s_z.sem, s_z.at(b, c + 1))
                    for t in range(TC):
                        last = nc.tensor.transpose(dst[:, t * P:(t + 1) * P],
                                                   att[:, c * TC + t, k * P:(k + 1) * P], ident[:, :])
                    last.then_inc(x_full.sem, 1)

            def second_mlp(b):
                for c in range(NC):
                    dst = x_room(b, "r2", c)
                    pe.wait_ge(x_dve.sem, x_dve.at(b, XF.emptied(XF.index("zT", FK * (c + 1) - 1))))
                    for k in range(FK):
                        last = nc.tensor.matmul(dst[:, :], w2s[:, k, :], r1T[:, k, c * BANK:(c + 1) * BANK],
                                                start=(k == 0), stop=(k == FK - 1))
                    last.then_inc(x_full.sem, 1)

            def second_h(b):
                for n in range(NT // 2):
                    dst = x_room(b, "h2", n)
                    emptied_act(b, "r2", 2 * n // TC)
                    for t in range(2):
                        jt = 2 * n + t
                        last = nc.tensor.matmul(dst[:, t * HW:(t + 1) * HW], r2T[:, jt * P:(jt + 1) * P], whx[:, :],
                                                start=True, stop=True)
                    last.then_inc(x_full.sem, 1)

            def mean_h(b):
                dst = x_room(b, "hm")
                pe.wait_ge(s_bc.sem, s_bc.at(b, 2))
                nc.tensor.matmul(dst[:, 0:D], r2bc[:, :], whx[:, 1:HW], start=True, stop=True).then_inc(x_full.sem, 1)

            def att2(b, first, end):
                for m in range(first, end):
                    it, jt = m // NT, m % NT
                    t = it % 2
                    if t == 0 and jt == 0:
                        x_room(b, "att2", it // 2)
                    if it == 0:
                        pe.wait_ge(s_p2.sem, s_p2.at(b, jt + 1))
                    last = nc.tensor.matmul(px[XF.index("att2", it // 2) % 2][:, t * HW:(t + 1) * HW],
                                            pw[:, jt, it * P:(it + 1) * P], h2x[:, jt, 1:HW + 1],
                                            start=(jt == 0), stop=(jt == NT - 1))
                    if t == 1 and jt == NT - 1:
                        last.then_inc(x_full.sem, 1)

            def turn_r2(b):
                for c in range(NC):
                    dst = x_room(b, "r2n", c)
                    for t in range(TC):
                        n = c * TC + t
                        last = nc.tensor.transpose(dst[:, t * P:(t + 1) * P], r2T[:, n * P:(n + 1) * P], ident[:, :])
                    last.then_inc(x_full.sem, 1)

            def turn_x1(b):
                s_room(b, "x1T")
                dst = pair("x1T")
                pe.wait_ge(s_ln.sem, s_ln.at(b, LN_ALL))
                for t in range(NT):
                    last = nc.tensor.transpose(dst[:, t * P:(t + 1) * P], x1[:, t, :], ident[:, :])
                last.then_inc(s_full.sem, 1)

            def queries_or_keys(b, n, w):
                s_room(b, "qk", n)
                dst = pair("qk", n)
                pe.wait_ge(f_act.sem, f_act.at(b, SF.emptied(SF.index("x1T"))))
                for c in range(NC):
                    last = nc.tensor.matmul(dst[:, c * BANK:(c + 1) * BANK], w[:, :],
                                            x1T[:, c * BANK:(c + 1) * BANK], start=True, stop=True)
                last.then_inc(s_full.sem, 1)

            def values(b):
                s_room(b, "v")
                dst = pair("v")
                for jt in range(NT):
                    last = nc.tensor.matmul(dst[:, jt * P:(jt + 1) * P], x1T[:, jt * P:(jt + 1) * P], wvs[:, :],
                                            start=True, stop=True)
                last.then_inc(s_full.sem, 1)

            def scores(b, n):
                it, h = n // H, n % H
                s_room(b, "score", n)
                dst = pair("score", n)
                if it == 0:
                    pe.wait_ge(s_stack[h].sem, s_stack[h].at(b, 16 * 4))
                for c in range(NC):
                    last = nc.tensor.matmul(dst[:, c * BANK:(c + 1) * BANK], qst[:, h, it * P:(it + 1) * P],
                                            kst[:, h, c * BANK:(c + 1) * BANK], start=True, stop=True)
                last.then_inc(s_full.sem, 1)

            def turn(b, n):
                pe.wait_ge(s_den.sem, s_den.at(b, n + 1))
                for c in range(NC):
                    s_room(b, "turned", NC * n + c)
                    for t in range(TC):
                        jt = c * TC + t
                        last = nc.tensor.transpose(turned(n, c)[:, t * P:(t + 1) * P],
                                                   sm[:, n % NS, jt * P:(jt + 1) * P], ident[:, :])
                    last.then_inc(s_full.sem, 1)

            def products(b, p):
                last_kept = SF.index("turned", NC * ((p + 1) * 2 * H) - 1)
                pe.wait_ge(f_act.sem, f_act.at(b, SF.emptied(last_kept)))
                if p == TC // 2:
                    pe.wait_ge(s_oT.sem, s_oT.at(b, 1))
                columns = slice(2 * p % TC * P, (2 * p % TC + 2) * P)
                for jt in range(NT):
                    for h in range(H):
                        last = nc.tensor.matmul(po[h * HD:(h + 1) * HD, columns], vs[:, jt, h * HD:(h + 1) * HD],
                                                pt[:, kept_in(2 * p * H + h)[0], :, jt * P:(jt + 1) * P],
                                                start=(jt == 0), stop=(jt == NT - 1), tile_position=(0, h * HD))
                last.then_inc(s_pv.sem, 1)

            def heads_out(b):
                s_room(b, "on")
                dst = pair("on")
                pe.wait_ge(s_oT.sem, s_oT.at(b, NC))
                for it in range(NT):
                    last = nc.tensor.transpose(dst[:, it * P:(it + 1) * P], oT[:, it * P:(it + 1) * P], ident[:, :])
                last.then_inc(s_full.sem, 1)

            def turn_divided(b):
                s_room(b, "onT")
                dst = pair("onT")
                pe.wait_ge(f_dve.sem, f_dve.at(b, SF.emptied(SF.index("on"))))
                for it in range(NT):
                    last = nc.tensor.transpose(dst[:, it * P:(it + 1) * P], on[:, it, :], ident[:, :])
                last.then_inc(s_full.sem, 1)

            def projection(b):
                s_room(b, "proj")
                dst = pair("proj")
                pe.wait_ge(f_act.sem, f_act.at(b, SF.emptied(SF.index("onT"))))
                for it in range(NT):
                    last = nc.tensor.matmul(dst[:, it * P:(it + 1) * P], oT[:, it * P:(it + 1) * P], wos[:, :],
                                            start=True, stop=True)
                last.then_inc(s_full.sem, 1)

            def join(b1, b0, bh):
                if bh is not None:
                    turn_x(bh)
                if b1 is not None:
                    heads_out(b1)
                if bh is not None:
                    first_mlp(bh, 0)
                if b1 is not None:
                    turn_divided(b1)
                if bh is not None:
                    first_mlp(bh, 1)
                if b1 is not None:
                    projection(b1)
                if bh is not None:
                    first_h(bh)
                if b0 is not None:
                    turn_x1(b0)
                if bh is not None:
                    node_top(bh, 0)
                    f1_rows(bh, 0, [wa1[:, k, :] for k in range(FK)], [r1T[:, k, :] for k in range(FK)], 0)
                if b0 is not None:
                    queries_or_keys(b0, 0, wqs)
                if bh is not None:
                    f1_rows(bh, 0, [wa1[:, k, :] for k in range(FK)], [r1T[:, k, :] for k in range(FK)], 1)
                if b0 is not None:
                    queries_or_keys(b0, 1, wks)
                    values(b0)

            def middle(b1, b0):
                if b0 is not None:
                    att1(b0, 0, (AHEAD - 1) * NT)
                for n in range(LEAD):
                    if b1 is not None:
                        scores(b1, n)
                    if b0 is not None:
                        att1(b0, (AHEAD - 1) * NT + n * NT // LEAD, (AHEAD - 1) * NT + (n + 1) * NT // LEAD)
                for u in range(UNITS):
                    if b1 is not None and u + LEAD < UNITS:
                        scores(b1, u + LEAD)
                    if b0 is not None:
                        att1(b0, att1_through(u - 1) if u else AHEAD * NT, att1_through(u))
                        if u == Z_AT:
                            turn_z(b0, 0, FK * NC)
                        if u == R2_AT:
                            second_mlp(b0)
                        if u == H2_AT:
                            second_h(b0)
                        if u == F2_AT:
                            mean_h(b0)
                            node_top(b0, 1)
                            for c in range(NC):
                                f1_rows(b0, 1, [wh1[:, :]], [r2T[:, :]], c)
                        if u == R2N_AT:
                            turn_r2(b0)
                        att2(b0, att2_through(u - 1), att2_through(u))
                    if b1 is not None:
                        turn(b1, u)
                        if u and u % (2 * H) == 0:
                            products(b1, u // (2 * H) - 1)
                if b0 is not None:
                    att2(b0, att2_through(UNITS - 1), NT * NT)
                if b1 is not None:
                    products(b1, NT // 2 - 1)

            join(None, None, 0)
            pe.wait_ge(s_linked.sem, NT)
            for jt in range(NT):
                if jt >= 4:
                    pe.wait_ge(s_mtc.sem, jt - 3)
                for it in range(NT):
                    last = nc.tensor.transpose(setup_bank(jt).bitcast(BF16)[:, it * P:(it + 1) * P],
                                               linked[:, it, jt * P:(jt + 1) * P], identb[:, :])
                last.then_inc(s_mtr.sem, 1)
            middle(None, 0)
            pe.wait_ge(s_mtc.sem, NT)
            join(None, 0, 1)
            with pe.Fori(0, B - 2) as b:
                middle(b, b + 1)
                join(b, b + 1, b + 2)
            middle(B - 2, B - 1)
            join(B - 2, B - 1, None)
            middle(B - 1, None)
            join(B - 1, None, None)


def kernel(x, adj, L0_gnn_mlp1_w, L0_gnn_mlp1_b, L0_gnn_mlp2_w, L0_gnn_mlp2_b, L0_gnn_W_fc, L0_gnn_a_fc,
           L0_gnn_W_hand, L0_gnn_a_hand, L1_gnn_wq, L1_gnn_bq, L1_gnn_wk, L1_gnn_bk, L1_gnn_wv, L1_gnn_bv,
           L1_gnn_wo, L1_gnn_bo):
    import numpy as np
    import concourse.bacc as bacc
    from concourse.bass_utils import run_bass_kernel_spmd

    def rows(a):
        return np.tile(np.asarray(a)[None, :], (P, 1))

    def columns(a):
        return np.asarray(a).reshape(-1, P).T

    def turned(a):
        return np.asarray(a).T

    given = [
        ("x", x), ("adj", adj), ("w1", L0_gnn_mlp1_w), ("b1", columns(L0_gnn_mlp1_b)), ("w2", L0_gnn_mlp2_w),
        ("b2", L0_gnn_mlp2_b), ("wfc", L0_gnn_W_fc), ("wfcT", turned(L0_gnn_W_fc)),
        ("afc", np.asarray(L0_gnn_a_fc).reshape(2, -1, P).transpose(2, 1, 0)), ("wh", L0_gnn_W_hand), ("whT", turned(L0_gnn_W_hand)),
        ("ah", columns(L0_gnn_a_hand)), ("wqT", turned(L1_gnn_wq)), ("bq", L1_gnn_bq),
        ("wkT", turned(L1_gnn_wk)), ("bk", L1_gnn_bk), ("wvT", turned(L1_gnn_wv)), ("bv", rows(L1_gnn_bv)),
        ("woT", turned(L1_gnn_wo)), ("bo", rows(L1_gnn_bo)), ("eye", np.eye(P, dtype=np.float32)),
    ]
    nc = bacc.Bacc("TRN2", target_bir_lowering=False, num_devices=1)
    arrays, args = {}, []
    for name, a in given:
        a = np.ascontiguousarray(a)
        arrays[f"in_{name}"] = a
        args.append(nc.dram_tensor(f"in_{name}", a.shape, mybir.dt.from_np(a.dtype), kind="ExternalInput").ap())
    shape = arrays["in_x"].shape
    args.append(nc.dram_tensor("out_y", shape, F32, kind="ExternalOutput").ap())
    build(nc, *args)
    r = run_bass_kernel_spmd(nc, [arrays], core_ids=[0])
    return r.results[0]["out_y"]
```
